# Optimizing a Trainium2 kernel written in Bass

```python
import numpy as np
import jax
import jax.numpy as jnp

def _softmax(x, axis=-1):
    return jax.nn.softmax(x, axis=axis)

def _gelu(x):
    return jax.nn.gelu(x, approximate=True)

def _silu(x):
    return jax.nn.silu(x)

def _sigmoid(x):
    return jax.nn.sigmoid(x)

def _layernorm(x, axis=-1, eps=1e-05):
    m = jnp.mean(x, axis=axis, keepdims=True)
    v = jnp.var(x, axis=axis, keepdims=True)
    return (x - m) / jnp.sqrt(v + eps)

def _scatter_add(tgt, idx, src, axis=0):
    return tgt.at[idx].add(src)

def _segment_sum(src, seg, n):
    return jax.ops.segment_sum(src, seg, n)
kernel_name = 'mk_vit_tower_d1_tok_img1024_r4_af83e9'

def setup_inputs(seed: int=0):
    np.random.seed(seed)
    _w = jnp.asarray

    def _rec_inputs():
        import jax
        import jax.numpy as jnp
        _rk = jax.random.key(seed)
        x = -0.000392918 + 0.999932 * jax.random.normal(jax.random.fold_in(_rk, 1), (8, 256, 256, 1), jnp.float32)
        return x
    x = _rec_inputs()

    def _L0_tok_setup():
        import jax, jax.numpy as jnp
        import numpy as np
        INV_SQRT2 = 0.7071067811865476
        LEVEL = 3

        def _split(x, axis):
            ax = axis % x.ndim
            sl0 = [slice(None)] * x.ndim
            sl0[ax] = slice(0, None, 2)
            sl1 = [slice(None)] * x.ndim
            sl1[ax] = slice(1, None, 2)
            x0, x1 = (x[tuple(sl0)], x[tuple(sl1)])
            return ((x0 + x1) * INV_SQRT2, (x0 - x1) * INV_SQRT2)

        def _merge(lo, hi, axis):
            ax = axis % lo.ndim
            e = (lo + hi) * INV_SQRT2
            o = (lo - hi) * INV_SQRT2
            s = jnp.stack([e, o], axis=ax + 1)
            shape = list(lo.shape)
            shape[ax] *= 2
            return s.reshape(shape)

        def _dwt2(x):
            lo, hi = _split(x, -1)
            a, h = _split(lo, -2)
            v, d = _split(hi, -2)
            return (a, h, v, d)

        def _idwt2(a, h, v, d):
            lo = _merge(a, h, -2)
            hi = _merge(v, d, -2)
            return _merge(lo, hi, -1)
        key = jax.random.key(seed)
        ks = jax.random.split(key, 8)
        B, H, W = (16, 256, 256)
        x = jax.random.normal(ks[0], (B, H, W, 1), dtype=jnp.float32)
        na = H // 8 * (W // 8)
        n2 = H // 4 * (W // 4)
        n1 = H // 2 * (W // 2)
        scale = 0.02
        Wa = jax.random.normal(ks[1], (na, 1), dtype=jnp.float32) * scale
        ba = jnp.zeros((1,), jnp.float32)
        Wd1 = jax.random.normal(ks[2], (3 * na, 3), dtype=jnp.float32) * scale
        bd1 = jnp.zeros((3,), jnp.float32)
        Wd2 = jax.random.normal(ks[3], (3 * n2, 3), dtype=jnp.float32) * scale
        bd2 = jnp.zeros((3,), jnp.float32)
        Wd3 = jax.random.normal(ks[4], (3 * n1, 3), dtype=jnp.float32) * scale
        bd3 = jnp.zeros((3,), jnp.float32)
        return {'x': x, 'Wa': Wa, 'ba': ba, 'Wd1': Wd1, 'bd1': bd1, 'Wd2': Wd2, 'bd2': bd2, 'Wd3': Wd3, 'bd3': bd3}
    _L0_tok_all = _L0_tok_setup()
    _L0_tok_in = {k: v for k, v in _L0_tok_all.items() if k in ('Wa', 'ba', 'Wd1', 'bd1', 'Wd2', 'bd2', 'Wd3', 'bd3')}
    del _L0_tok_all

    def _L0_attn_setup():
        import jax, jax.numpy as jnp
        import numpy as np
        NUM_HEADS = 16
        key = jax.random.key(seed)
        ks = jax.random.split(key, 11)
        B, S, D = (4, 256, 256)
        M = 128
        hd = D // NUM_HEADS
        s = 0.02
        return {'x': jax.random.normal(ks[0], (B, S, D), jnp.float32), 'Wq': jax.random.normal(ks[1], (D, D), jnp.float32) * s, 'bq': jax.random.normal(ks[2], (D,), jnp.float32) * s, 'Wk': jax.random.normal(ks[3], (D, D), jnp.float32) * s, 'bk': jax.random.normal(ks[4], (D,), jnp.float32) * s, 'Wv': jax.random.normal(ks[5], (D, D), jnp.float32) * s, 'bv': jax.random.normal(ks[6], (D,), jnp.float32) * s, 'Wo': jax.random.normal(ks[7], (D, D), jnp.float32) * s, 'bo': jax.random.normal(ks[8], (D,), jnp.float32) * s, 'rel_k': jax.random.normal(ks[9], (2 * M + 1, hd), jnp.float32), 'rel_v': jax.random.normal(ks[10], (2 * M + 1, hd), jnp.float32)}
    _L0_attn_all = _L0_attn_setup()
    _L0_attn_in = {k: v for k, v in _L0_attn_all.items() if k in ('Wq', 'bq', 'Wk', 'bk', 'Wv', 'bv', 'Wo', 'bo', 'rel_k', 'rel_v')}
    del _L0_attn_all

    def _L0_ffn_setup():
        import jax, jax.numpy as jnp
        import numpy as np
        DIM = 256
        HIDDEN = 1024
        E = 8
        B, S = (2, 1024)
        key = jax.random.key(seed)
        ks = jax.random.split(key, 8)
        sd = 1.0 / np.sqrt(DIM)
        sh = 1.0 / np.sqrt(HIDDEN)
        return {'x': jax.random.normal(ks[0], (B, S, DIM), dtype=jnp.float32), 'router_w': jax.random.uniform(ks[1], (DIM, E), jnp.float32, -sd, sd), 'router_b': jax.random.uniform(ks[2], (E,), jnp.float32, -sd, sd), 'w1': jax.random.uniform(ks[3], (E, DIM, 2 * HIDDEN), jnp.float32, -sd, sd), 'b1': jax.random.uniform(ks[4], (E, 2 * HIDDEN), jnp.float32, -sd, sd), 'w2': jax.random.uniform(ks[5], (E, HIDDEN, DIM), jnp.float32, -sh, sh), 'b2': jax.random.uniform(ks[6], (E, DIM), jnp.float32, -sh, sh)}
    _L0_ffn_all = _L0_ffn_setup()
    _L0_ffn_in = {k: v for k, v in _L0_ffn_all.items() if k in ('router_w', 'router_b', 'w1', 'b1', 'w2', 'b2')}
    del _L0_ffn_all
    return {'x': x, 'L0_tok_Wa': _L0_tok_in['Wa'], 'L0_tok_ba': _L0_tok_in['ba'], 'L0_tok_Wd1': _L0_tok_in['Wd1'], 'L0_tok_bd1': _L0_tok_in['bd1'], 'L0_tok_Wd2': _L0_tok_in['Wd2'], 'L0_tok_bd2': _L0_tok_in['bd2'], 'L0_tok_Wd3': _L0_tok_in['Wd3'], 'L0_tok_bd3': _L0_tok_in['bd3'], 'L0_attn_Wq': _L0_attn_in['Wq'], 'L0_attn_bq': _L0_attn_in['bq'], 'L0_attn_Wk': _L0_attn_in['Wk'], 'L0_attn_bk': _L0_attn_in['bk'], 'L0_attn_Wv': _L0_attn_in['Wv'], 'L0_attn_bv': _L0_attn_in['bv'], 'L0_attn_Wo': _L0_attn_in['Wo'], 'L0_attn_bo': _L0_attn_in['bo'], 'L0_attn_rel_k': _L0_attn_in['rel_k'], 'L0_attn_rel_v': _L0_attn_in['rel_v'], 'L0_ffn_router_w': _L0_ffn_in['router_w'], 'L0_ffn_router_b': _L0_ffn_in['router_b'], 'L0_ffn_w1': _L0_ffn_in['w1'], 'L0_ffn_b1': _L0_ffn_in['b1'], 'L0_ffn_w2': _L0_ffn_in['w2'], 'L0_ffn_b2': _L0_ffn_in['b2']}

def reference(x, L0_tok_Wa, L0_tok_ba, L0_tok_Wd1, L0_tok_bd1, L0_tok_Wd2, L0_tok_bd2, L0_tok_Wd3, L0_tok_bd3, L0_attn_Wq, L0_attn_bq, L0_attn_Wk, L0_attn_bk, L0_attn_Wv, L0_attn_bv, L0_attn_Wo, L0_attn_bo, L0_attn_rel_k, L0_attn_rel_v, L0_ffn_router_w, L0_ffn_router_b, L0_ffn_w1, L0_ffn_b1, L0_ffn_w2, L0_ffn_b2):
    import jax
    import jax.numpy as jnp

    def _L0_tok_ref(x, Wa, ba, Wd1, bd1, Wd2, bd2, Wd3, bd3):
        import jax, jax.numpy as jnp
        import numpy as np
        INV_SQRT2 = 0.7071067811865476
        LEVEL = 3

        def _split(x, axis):
            ax = axis % x.ndim
            sl0 = [slice(None)] * x.ndim
            sl0[ax] = slice(0, None, 2)
            sl1 = [slice(None)] * x.ndim
            sl1[ax] = slice(1, None, 2)
            x0, x1 = (x[tuple(sl0)], x[tuple(sl1)])
            return ((x0 + x1) * INV_SQRT2, (x0 - x1) * INV_SQRT2)

        def _merge(lo, hi, axis):
            ax = axis % lo.ndim
            e = (lo + hi) * INV_SQRT2
            o = (lo - hi) * INV_SQRT2
            s = jnp.stack([e, o], axis=ax + 1)
            shape = list(lo.shape)
            shape[ax] *= 2
            return s.reshape(shape)

        def _dwt2(x):
            lo, hi = _split(x, -1)
            a, h = _split(lo, -2)
            v, d = _split(hi, -2)
            return (a, h, v, d)

        def _idwt2(a, h, v, d):
            lo = _merge(a, h, -2)
            hi = _merge(v, d, -2)
            return _merge(lo, hi, -1)
        img = x[..., 0]
        B = img.shape[0]
        details = []
        cur = img
        for _ in range(LEVEL):
            cur, h, v, d = _dwt2(cur)
            details.append((h, v, d))
        aw = jax.nn.sigmoid(cur.reshape(B, -1) @ Wa + ba)
        rec = cur * aw[:, :, None]
        det_params = [(Wd1, bd1), (Wd2, bd2), (Wd3, bd3)]
        for (h, v, d), (Wd, bd) in zip(reversed(details), det_params):
            flat = jnp.stack([h, v, d], axis=1).reshape(B, -1)
            w = jax.nn.softmax(flat @ Wd + bd, axis=-1)
            rec = _idwt2(rec, h * w[:, 0, None, None], v * w[:, 1, None, None], d * w[:, 2, None, None])
        return rec

    def _L0_attn_ref(x, Wq, bq, Wk, bk, Wv, bv, Wo, bo, rel_k, rel_v):
        import jax, jax.numpy as jnp
        import numpy as np
        NUM_HEADS = 16
        B, S, D = x.shape
        H = NUM_HEADS
        hd = D // H
        M = (rel_k.shape[0] - 1) // 2

        def proj(W, b):
            return (x @ W.T + b).reshape(B, S, H, hd).transpose(0, 2, 1, 3)
        q = proj(Wq, bq)
        k = proj(Wk, bk)
        v = proj(Wv, bv)
        r = jnp.arange(S)
        idx = jnp.clip(r[None, :] - r[:, None], -M, M) + M
        rpk = rel_k[idx]
        rpv = rel_v[idx]
        content = jnp.einsum('bhqd,bhkd->bhqk', q, k)
        relative = jnp.einsum('bhqd,qkd->bhqk', q, rpk)
        scores = (content + relative) / jnp.sqrt(jnp.float32(hd))
        w = jax.nn.softmax(scores, axis=-1)
        out = jnp.einsum('bhqk,bhkd->bhqd', w, v) + jnp.einsum('bhqk,qkd->bhqd', w, rpv)
        out = out.transpose(0, 2, 1, 3).reshape(B, S, D)
        return out @ Wo.T + bo

    def _L0_ffn_ref(x, router_w, router_b, w1, b1, w2, b2):
        import jax, jax.numpy as jnp
        import numpy as np
        DIM = 256
        HIDDEN = 1024
        E = 8
        B, S = (2, 1024)
        logits = jnp.einsum('bsd,de->bse', x, router_w) + router_b
        probs = jax.nn.softmax(logits, axis=-1)
        top1 = jnp.argmax(probs, axis=-1)
        out = jnp.zeros_like(x)
        for i in range(E):
            h = jnp.einsum('bsd,df->bsf', x, w1[i]) + b1[i]
            a, g = jnp.split(h, 2, axis=-1)
            y = jnp.einsum('bsh,hd->bsd', a * jax.nn.sigmoid(g), w2[i]) + b2[i]
            out = out + jnp.where((top1 == i)[..., None], y, 0.0)
        return out
    h = _L0_tok_ref(x, L0_tok_Wa, L0_tok_ba, L0_tok_Wd1, L0_tok_bd1, L0_tok_Wd2, L0_tok_bd2, L0_tok_Wd3, L0_tok_bd3)
    h = h + _L0_attn_ref(_layernorm(h, axis=-1), L0_attn_Wq, L0_attn_bq, L0_attn_Wk, L0_attn_bk, L0_attn_Wv, L0_attn_bv, L0_attn_Wo, L0_attn_bo, L0_attn_rel_k, L0_attn_rel_v)
    h = h + _L0_ffn_ref(_layernorm(h, axis=-1), L0_ffn_router_w, L0_ffn_router_b, L0_ffn_w1, L0_ffn_b1, L0_ffn_w2, L0_ffn_b2)
    return h

_drawn_inputs = setup_inputs


def setup_inputs(seed=0):
    import zlib

    import numpy as np

    out = dict(_drawn_inputs(seed))
    spreads = {'L0_tok_bd1': (0.0, 0.1), 'L0_tok_bd2': (0.0, 0.1), 'L0_tok_bd3': (0.0, 0.279)}
    factors = {'L0_attn_bq': 3.902, 'L0_attn_bk': 8.0, 'L0_ffn_b1': 2.782}
    for name, (base, spread) in spreads.items():
        noise = np.random.default_rng([zlib.crc32(name.encode()), seed]).standard_normal(out[name].shape)
        drawn = base * np.exp(spread * noise) if base else spread * noise
        out[name] = jnp.asarray(drawn.astype(out[name].dtype))
    for name, factor in factors.items():
        out[name] = (out[name] * factor).astype(out[name].dtype)
    return out
```

```python
import numpy as np
from contextlib import ExitStack

import concourse.bass as bass
from concourse import mybir

F32 = mybir.dt.float32
F32R = mybir.dt.float32r
BF16 = mybir.dt.bfloat16
F16 = mybir.dt.float16
I32 = mybir.dt.int32
U32 = mybir.dt.uint32
ALU = mybir.AluOpType
ACT = mybir.ActivationFunctionType
AX = mybir.AxisListType

P = 128
B, S, D = 8, 256, 256
TOK = B * S
TT = TOK // P
KC = D // P
HEADS, HD = 16, 16
EXPERTS, HID = 8, 1024
EPS = 1e-5
LEVELS = 3
ROWS = 8
HALF = 2
NPART = 3
Q_TERMS = (0, 0, 1, 1, 0, 2)
K_TERMS = (0, 1, 0, 1, 2, 0)
STACK = len(Q_TERMS) * HD
EXT = 512
WQ = 64
NWIN = S // WQ
BG = 4
GROUPS = B // BG
WINDOWS = GROUPS * NWIN


def wavelet_columns():
    at, found = 1, {0: (0, ROWS * D >> (2 * LEVELS))}
    at = found[0][1]
    for level in range(LEVELS, 0, -1):
        n = 3 * (ROWS * D >> (2 * level))
        found[level] = (at, n)
        at += 3 * n
    return found, at


def tokens_stage(nc, x, wave_w, wave_b, wq_t, wk_t, wv_t, qkv_b, ext_k, ext_v, h_dram, v_parts, q_dram, k_dram,
                 ek_dram, ev_dram, rx_dram, ident):
    columns, wave_n = wavelet_columns()
    with ExitStack() as ctx:
        def sb(name, shape, dt=F32):
            return ctx.enter_context(nc.sbuf_tensor(name, shape, dt))

        def sem(name):
            return ctx.enter_context(nc.semaphore(name))

        img = sb("img", [P, HALF, ROWS * D])
        wave = sb("wave", [P, wave_n])
        wbias = sb("wbias", [P, 10])
        blocks = sb("blocks", [P, 4, 32])
        band = {n: sb(f"band{n}", [P, HALF, 4, ROWS * D >> (2 * n)]) for n in (1, 2, 3)}
        mix = sb("mix", [P, HALF, 2, ROWS * D // 2])
        junk = sb("junk", [P, 3 * ROWS * D // 4])
        dots = sb("dots", [P, HALF, 10])
        z = sb("z", [P, HALF, 10])
        zmax = sb("zmax", [P, HALF, 3])
        e = sb("e", [P, HALF, 10])
        esum = sb("esum", [P, HALF, 4])
        einv = sb("einv", [P, HALF, 4])
        gate = sb("gate", [P, HALF, 10])
        stats = sb("stats", [P, TT, 6])
        mv = sb("mv", [P, TT, 2])
        var = sb("var", [P, TT])
        sd = sb("sd", [P, TT])
        rs = sb("rs", [P, 4, TT])
        xnt = sb("xnt", [P, KC, TOK])
        wqk = sb("wqk", [P, 2, KC, D])
        wv = sb("wv", [P, KC, D])
        qk_b = sb("qk_b", [P, 2, KC])
        v_b = sb("v_b", [P, D])
        full = sb("full", [P, 2, 512])
        rest = sb("rest", [P, 2, 512])
        parts = sb("parts", [P, 2, NPART, 512], BF16)
        vfull = sb("vfull", [P, 2, D])
        vrest = sb("vrest", [P, 2, D])
        ek = sb("ek", [HD, EXT])
        ek3 = sb("ek3", [HD, NPART, EXT], BF16)
        ev = sb("ev", [P, EXT * HD // P])
        ev3 = sb("ev3", [P, EXT // P, NPART, HD], BF16)
        h_sb = sb("h_sb", [P, HALF, ROWS, D])
        ps_dots = ctx.enter_context(nc.psum_tensor("ps_dots", [P, 512], F32))
        ps_t = ctx.enter_context(nc.psum_tensor("ps_t", [P, 2, 512], F32))
        ps_p = ctx.enter_context(nc.psum_tensor("ps_p", [P, 2, 512], F32))
        ps_v = ctx.enter_context(nc.psum_tensor("ps_v", [P, 2, 512], F32))

        x_in = [sem(f"x_in{t}") for t in range(HALF)]
        wave_in = sem("wave_in")
        w_in = sem("w_in")
        ext_in = sem("ext_in")
        const_done = sem("const_done")
        haar = sem("haar")
        dots_done = sem("dots_done")
        dots_summed = sem("dots_summed")
        exp_ready = sem("exp_ready")
        exp_done = sem("exp_done")
        gate_ready = sem("gate_ready")
        scaled = sem("scaled")
        var_ready = sem("var_ready")
        sd_done = sem("sd_done")
        norm_done = sem("norm_done")
        turned = sem("turned")
        turned_out = sem("turned_out")
        proj_done = sem("proj_done")
        full_done = sem("full_done")
        split_done = sem("split_done")
        parts_sent = [sem(f"parts_sent{i}") for i in range(2)]
        vproj_done = sem("vproj_done")
        vhigh_done = sem("vhigh_done")
        v_step = sem("v_step")
        h_sent = sem("h_sent")
        ext_split = sem("ext_split")
        ext_step = sem("ext_step")
        ext_sent = sem("ext_sent")

        block = ctx.enter_context(nc.Block())
        rows_v = x.rearrange("b (r j) c o -> (b r) (j c o)", j=ROWS)
        NS = TOK // 512
        slices = [(m, c, s) for s in range(NS) for m in range(2) for c in range(KC)]

        @block.sync
        def _(sp):
            for t in range(HALF):
                sp.dma_start(img[:, t, :], rows_v[t * P:(t + 1) * P, :]).then_inc(x_in[t], 16)
            for i in range(4):
                sp.dma_start(wave[32 * i:32 * i + 32, :], wave_w).then_inc(wave_in, 16)
            sp.dma_start(wbias[:, :], wave_b.rearrange("(a n) -> a n", a=1).broadcast_to([P, 10])).then_inc(wave_in, 16)
            sp.dma_start(ek[:, :], ext_k).then_inc(ext_in, 16)
            sp.dma_start(ev[:, :], ext_v.rearrange("(p n) d -> p (n d)", p=P)).then_inc(ext_in, 16)
            for m, w in enumerate((wq_t, wk_t)):
                sp.dma_start(wqk[:, m, :, :], w.rearrange("(k p) n -> p k n", p=P)).then_inc(w_in, 16)
            sp.dma_start(wv[:, :, :], wv_t.rearrange("(k p) n -> p k n", p=P)).then_inc(w_in, 16)
            for m in range(2):
                sp.dma_start(qk_b[:, m, :], qkv_b[m].rearrange("(k p) -> p k", p=P),
                             allow_slow_non_contiguous=True).then_inc(w_in, 16)
            sp.dma_start(v_b[:, :], qkv_b[2:3, :].broadcast_to([P, D])).then_inc(w_in, 16)
            sp.wait_ge(norm_done, 1)
            sp.dma_start(h_dram.rearrange("(t p j) c -> p t j c", t=HALF, j=ROWS), h_sb[:, :, :, :]).then_inc(h_sent, 16)
            sp.wait_ge(ext_split, 2)
            for t in range(len(K_TERMS)):
                sp.dma_start(ek_dram[t * HD:(t + 1) * HD, :], ek3[:, K_TERMS[t], :]).then_inc(ext_sent, 16)
            sp.dma_start(ev_dram.rearrange("(p n) a d -> p n a d", p=P), ev3[:, :, :, :]).then_inc(ext_sent, 16)
            row = NPART * HD
            sp.wait_ge(ext_sent, 16 * (len(K_TERMS) + 1))
            for w in range(NWIN):
                for c in range(KC):
                    sp.dma_start(rx_dram[w, c],
                                 bass.AP(ev_dram.tensor, (c * P + S - (w + 1) * WQ) * row, [[row, P], [1, WQ * row]])
                                 ).then_inc(ext_sent, 16)
            sent = [0, 0]
            for i, (m, c, s) in enumerate(slices):
                sp.wait_ge(split_done, i + 1)
                rows = slice(c * P, (c + 1) * P)
                for n in range(NPART):
                    if m:
                        sp.dma_start(k_dram[n, rows, 2 * s:2 * s + 2, :].rearrange("r b k -> r (b k)"),
                                     parts[:, i % 2, n, :]).then_inc(parts_sent[i % 2], 16)
                        sent[i % 2] += 1
                        continue
                    for b in (2 * s, 2 * s + 1):
                        first = NWIN * (b // BG)
                        sp.dma_start(q_dram[first:first + NWIN, n, rows, b % BG, :].rearrange("w r q -> r w q"),
                                     parts[:, i % 2, n, (b % 2) * S:(b % 2 + 1) * S].rearrange(
                                         "p (w q) -> p w q", q=WQ)).then_inc(parts_sent[i % 2], 16)
                        sent[i % 2] += 1
            sp.wait_ge(h_sent, 16)
            for i in range(2):
                sp.wait_ge(parts_sent[i], 16 * sent[i])
            sp.wait_ge(ext_sent, 16 * (len(K_TERMS) + 1 + NWIN * KC))

        @block.gpsimd
        def _(pool):
            pool.memset(ident[:, :], 0.0).then_inc(const_done, 1)
            pool.memset(blocks[:, :, :], 1.0).then_inc(const_done, 1)
            pool.wait_ge(const_done, 2)
            pool.affine_select(out=ident[:, :], in_=ident[:, :], compare_op=ALU.not_equal, fill=1.0, base=0,
                               pattern=[[-1, P]], channel_multiplier=1).then_inc(const_done, 1)
            pool.affine_select(out=blocks[:, :, :], in_=blocks[:, :, :], compare_op=ALU.is_ge, fill=0.0, base=0,
                               pattern=[[-32, 4], [0, 32]], channel_multiplier=1).then_inc(const_done, 1)
            pool.wait_ge(const_done, 4)
            pool.affine_select(out=blocks[:, :, :], in_=blocks[:, :, :], compare_op=ALU.is_ge, fill=0.0, base=31,
                               pattern=[[32, 4], [0, 32]], channel_multiplier=-1).then_inc(const_done, 1)

        @block.vector
        def _(dve):
            n_haar = [0]

            def stepped(ins):
                n_haar[0] += 1
                ins.then_inc(haar, 1)
                return n_haar[0]

            def source(level, t):
                return img[:, t, :] if level == 1 else band[level - 1][:, t, 0, :]

            dve.wait_ge(wave_in, 16 * 5)
            for t in range(HALF):
                dve.wait_ge(x_in[t], 16)
                for level in (1, 2, 3):
                    n = ROWS * D >> (2 * level - 2)
                    cols = D >> level
                    pair = source(level, t).rearrange("p (n two) -> p n two", two=2)
                    m = mix[:, t, :, 0:n // 2]
                    stepped(dve.tensor_tensor(m[:, 0, :], pair[:, :, 0], pair[:, :, 1], ALU.add))
                    dve.wait_ge(haar, stepped(dve.tensor_tensor(m[:, 1, :], pair[:, :, 0], pair[:, :, 1], ALU.subtract)))
                    m4 = m.rearrange("p a (r two c) -> p a r two c", two=2, c=cols)
                    out = band[level][:, t, :, :].rearrange("p a (r c) -> p a r c", c=cols)
                    stepped(dve.tensor_tensor(out[:, 0:4:2], m4[:, :, :, 0, :], m4[:, :, :, 1, :], ALU.add))
                    dve.wait_ge(haar, stepped(dve.tensor_tensor(out[:, 1:4:2], m4[:, :, :, 0, :], m4[:, :, :, 1, :],
                                                                ALU.subtract)))
                at, n = columns[0]
                dve.wait_ge(haar, stepped(dve.tensor_tensor_reduce(
                    junk[:, 0:n], band[3][:, t, 0, :], wave[:, at:at + n], 0.5 ** LEVELS, 0.0, ALU.mult, ALU.add,
                    dots[:, t, 0:1])))
                for level in (3, 2, 1):
                    at, n = columns[level]
                    for c in range(3):
                        col = 1 + 3 * (3 - level) + c
                        dve.wait_ge(haar, stepped(dve.tensor_tensor_reduce(
                            junk[:, 0:n], band[level][:, t, 1:4, :].rearrange("p a n -> p (a n)"),
                            wave[:, at + c * n:at + (c + 1) * n], 0.5 ** level, 0.0, ALU.mult, ALU.add,
                            dots[:, t, col:col + 1])))
            dve.engine_nop().then_inc(dots_done, 1)
            dve.wait_ge(dots_summed, 1)
            s1 = stepped(dve.tensor_tensor(z[:, :, :], ps_dots[:, 0:20].rearrange("p (t n) -> p t n", t=HALF),
                                           wbias[:, :].unsqueeze(1).broadcast_to([P, HALF, 10]), ALU.add))
            dve.wait_ge(haar, s1)
            z3 = z[:, :, 1:10].rearrange("p t (l c) -> p t l c", c=3)
            e3 = e[:, :, 1:10].rearrange("p t (l c) -> p t l c", c=3)
            dve.wait_ge(haar, stepped(dve.tensor_reduce(zmax[:, :, :], z3, AX.X, ALU.max)))
            for t in range(HALF):
                stepped(dve.tensor_tensor(z3[:, t], z3[:, t], zmax[:, t, :].unsqueeze(2).broadcast_to([P, 3, 3]), ALU.subtract))
            dve.wait_ge(haar, stepped(dve.tensor_scalar(z[:, :, 0:1], z[:, :, 0:1], -1.0, None, ALU.mult)))
            dve.engine_nop().then_inc(exp_ready, 1)
            dve.wait_ge(exp_done, 1)
            stepped(dve.tensor_reduce(esum[:, :, 1:4], e3, AX.X, ALU.add))
            dve.wait_ge(haar, stepped(dve.tensor_scalar(esum[:, :, 0:1], e[:, :, 0:1], 1.0, None, ALU.add)))
            dve.wait_ge(haar, stepped(dve.reciprocal(einv[:, :, :], esum[:, :, :])))
            stepped(dve.tensor_scalar(gate[:, :, 0:1], einv[:, :, 0:1], 0.25 ** 3, None, ALU.mult))
            for t in range(HALF):
                for level in (3, 2, 1):
                    a = 1 + 3 * (3 - level)
                    k = stepped(dve.tensor_scalar(gate[:, t, a:a + 3], e[:, t, a:a + 3], einv[:, t, 4 - level:5 - level],
                                                  0.25 ** level, ALU.mult, ALU.mult))
            dve.wait_ge(haar, k)
            dve.engine_nop().then_inc(gate_ready, 1)
            for t in range(HALF):
                for level in (3, 2, 1):
                    dve.wait_ge(scaled, 10 * t + {3: 4, 2: 7, 1: 10}[level])
                    n = ROWS * D >> (2 * level - 2)
                    cols = D >> level
                    m = mix[:, t, :, 0:n // 2]
                    m4 = m.rearrange("p a (r two c) -> p a r two c", two=2, c=cols)
                    bd = band[level][:, t, :, :].rearrange("p a (r c) -> p a r c", c=cols)
                    stepped(dve.tensor_tensor(m4[:, :, :, 0, :], bd[:, 0:4:2], bd[:, 1:4:2], ALU.add))
                    dve.wait_ge(haar, stepped(dve.tensor_tensor(m4[:, :, :, 1, :], bd[:, 0:4:2], bd[:, 1:4:2],
                                                                ALU.subtract)))
                    out = h_sb[:, t, :, :].rearrange("p j c -> p (j c)") if level == 1 else band[level - 1][:, t, 0, :]
                    out = out.rearrange("p (n two) -> p n two", two=2)
                    stepped(dve.tensor_tensor(out[:, :, 0], m[:, 0, :], m[:, 1, :], ALU.add))
                    dve.wait_ge(haar, stepped(dve.tensor_tensor(out[:, :, 1], m[:, 0, :], m[:, 1, :], ALU.subtract)))
            for i in range(TT):
                k = stepped(dve.bn_stats(stats[:, i, :], h_sb[:, i // ROWS, i % ROWS, :]))
            dve.wait_ge(haar, k)
            for i in range(TT):
                k = stepped(dve.bn_aggr(mv[:, i, :], stats[:, i, :]))
            dve.wait_ge(haar, k)
            dve.wait_ge(haar, stepped(dve.tensor_scalar(var[:, :], mv[:, :, 1], EPS, None, ALU.add)))
            dve.engine_nop().then_inc(var_ready, 1)
            dve.wait_ge(sd_done, 1)
            dve.wait_ge(haar, stepped(dve.reciprocal(rs[:, 0, :], sd[:, :])))
            dve.wait_ge(haar, stepped(dve.tensor_tensor(rs[:, 1, :], rs[:, 0, :], rs[:, 0, :], ALU.mult)))
            dve.wait_ge(haar, stepped(dve.tensor_tensor(rs[:, 2, :], rs[:, 1, :], var[:, :], ALU.mult)))
            dve.wait_ge(haar, stepped(dve.tensor_scalar(rs[:, 1, :], rs[:, 2, :], -0.5, 1.5, ALU.mult, ALU.add)))
            dve.wait_ge(haar, stepped(dve.tensor_tensor(rs[:, 3, :], rs[:, 0, :], rs[:, 1, :], ALU.mult)))
            for i in range(TT):
                t, j = i // ROWS, i % ROWS
                dve.tensor_scalar(img[:, t, j * D:(j + 1) * D], h_sb[:, t, j, :], mv[:, i, 0:1], rs[:, 3, i:i + 1],
                                  ALU.subtract, ALU.mult).then_inc(norm_done, 1)
            dve.wait_ge(ext_in, 32)
            n_ext = 0
            ev_v = ev[:, :].rearrange("p (n d) -> p n d", d=HD)
            for full_ap, part_aps in ((ek[:, :], [ek3[:, n, :] for n in range(NPART)]),
                                      (ev_v, [ev3[:, :, n, :] for n in range(NPART)])):
                for n in range(NPART):
                    dve.tensor_copy(part_aps[n], full_ap).then_inc(ext_step, 1)
                    n_ext += 1
                    dve.wait_ge(ext_step, n_ext)
                    if n < NPART - 1:
                        dve.tensor_tensor(full_ap, full_ap, part_aps[n], ALU.subtract).then_inc(ext_step, 1)
                        n_ext += 1
                        dve.wait_ge(ext_step, n_ext)
                dve.engine_nop().then_inc(ext_split, 1)
            sent = [0, 0]
            for i, (m, c, s) in enumerate(slices):
                dve.wait_ge(full_done, 2 * (i + 1))
                if i >= 2:
                    dve.wait_ge(parts_sent[i % 2], 16 * sent[i % 2])
                sent[i % 2] += NPART * (1 if m else 2)
                dve.wait_ge(haar, stepped(dve.tensor_tensor(rest[:, i % 2, :], full[:, i % 2, :], parts[:, i % 2, 0, :],
                                                            ALU.subtract)))
                dve.wait_ge(haar, stepped(dve.tensor_copy(parts[:, i % 2, 1, :], rest[:, i % 2, :])))
                dve.tensor_tensor(parts[:, i % 2, 2, :], rest[:, i % 2, :], parts[:, i % 2, 1, :],
                                  ALU.subtract).then_inc(split_done, 1)
            for i in range(TT):
                b, c = i // KC, i % KC
                dve.wait_ge(vproj_done, i + 1)
                dve.tensor_tensor(vfull[:, i % 2, :], ps_v[:, i % 2, 0:D], v_b[:, :], ALU.add).then_inc(v_step, 1)
                dve.wait_ge(v_step, 4 * i + 1)
                dve.tensor_copy(v_parts[:, 0, c, b, :], vfull[:, i % 2, :]).then_inc(haar, 1)
                n_haar[0] += 1
                dve.wait_ge(haar, n_haar[0])
                dve.tensor_tensor(vrest[:, i % 2, :], vfull[:, i % 2, :], v_parts[:, 0, c, b, :],
                                  ALU.subtract).then_inc(v_step, 1)
                dve.wait_ge(v_step, 4 * i + 2)
                dve.tensor_copy(v_parts[:, 1, c, b, :], vrest[:, i % 2, :]).then_inc(v_step, 1)
                dve.wait_ge(v_step, 4 * i + 3)
                dve.tensor_tensor(v_parts[:, 2, c, b, :], vrest[:, i % 2, :], v_parts[:, 1, c, b, :],
                                  ALU.subtract).then_inc(v_step, 1)

        @block.scalar
        def _(act):
            act.wait_ge(exp_ready, 1)
            act.activation(e[:, :, :], z[:, :, :], ACT.Exp).then_inc(exp_done, 1)
            act.wait_ge(gate_ready, 1)
            for t in range(HALF):
                act.activation(band[3][:, t, 0, :], band[3][:, t, 0, :], ACT.Copy, scale=gate[:, t, 0:1]).then_inc(scaled, 1)
                for level in (3, 2, 1):
                    for c in range(3):
                        col = 1 + 3 * (3 - level) + c
                        act.activation(band[level][:, t, 1 + c, :], band[level][:, t, 1 + c, :], ACT.Copy,
                                       scale=gate[:, t, col:col + 1]).then_inc(scaled, 1)
            act.wait_ge(var_ready, 1)
            act.activation(sd[:, :], var[:, :], ACT.Sqrt).then_inc(sd_done, 1)
            xnt_v = xnt[:, :, :].rearrange("f k (t p j) -> f k t p j", t=HALF, j=ROWS)
            for i in range(TT // 2):
                t, j = 2 * i // ROWS, 2 * i % ROWS
                act.wait_ge(turned, i + 1)
                for jj in range(2):
                    ins = act.activation(xnt_v[:, :, t, :, j + jj],
                                   ps_t[:, i % 2, jj * D:(jj + 1) * D].rearrange("f (k p) -> f k p", k=KC),
                                   ACT.Copy)
                ins.then_inc(turned_out, 1)
            act.wait_ge(w_in, 16 * 6)
            for i, (m, c, s) in enumerate(slices):
                act.wait_ge(proj_done, i + 1)
                if i >= 2:
                    act.wait_ge(split_done, i - 1)
                act.activation(full[:, i % 2, :], ps_p[:, i % 2, :], ACT.Identity, bias=qk_b[:, m, c:c + 1]).then_inc(full_done, 1)
                if i >= 2:
                    need = NPART * sum(1 if slices[k][0] else 2 for k in range(i % 2, i, 2))
                    act.wait_ge(parts_sent[i % 2], 16 * need)
                act.activation(parts[:, i % 2, 0, :], ps_p[:, i % 2, :], ACT.Identity, bias=qk_b[:, m, c:c + 1]).then_inc(full_done, 1)

        @block.tensor
        def _(pe):
            pe.wait_ge(const_done, 5)
            pe.wait_ge(dots_done, 1)
            pe.matmul(ps_dots[:, 0:20], blocks[:, :, :].rearrange("p a b -> p (a b)"),
                      dots[:, :, :].rearrange("p t n -> p (t n)"), start=True, stop=True).then_inc(dots_summed, 1)
            for i in range(TT // 2):
                if i >= 2:
                    pe.wait_ge(turned_out, i - 1)
                for jj in range(2):
                    n = 2 * i + jj
                    pe.wait_ge(norm_done, n + 1)
                    for k in range(KC):
                        at = (n % ROWS) * D + k * P
                        ins = pe.transpose(ps_t[:, i % 2, jj * D + k * P:jj * D + (k + 1) * P],
                                           img[:, n // ROWS, at:at + P], ident[:, :])
                ins.then_inc(turned, 1)
            pe.wait_ge(turned_out, TT // 2)
            pe.wait_ge(w_in, 16 * 6)
            for i, (m, c, s) in enumerate(slices):
                if i >= 2:
                    pe.wait_ge(full_done, 2 * (i - 1))
                for k in range(KC):
                    ins = pe.matmul(ps_p[:, i % 2, :], wqk[:, m, k, c * P:(c + 1) * P], xnt[:, k, s * 512:(s + 1) * 512],
                                    start=(k == 0), stop=(k == KC - 1))
                ins.then_inc(proj_done, 1)
            for i in range(TT):
                if i >= 2:
                    pe.wait_ge(v_step, 4 * (i - 2) + 1)
                for k in range(KC):
                    ins = pe.matmul(ps_v[:, i % 2, 0:D], xnt[:, k, i * P:(i + 1) * P], wv[:, k, :],
                                    start=(k == 0), stop=(k == KC - 1))
                ins.then_inc(vproj_done, 1)


NB = BG * HEADS
TILES = NB // 2
SLOTS = 2
PAIRS = WQ // 2
EXTW = WQ - 1 + S + 1
SCALE = float(HD) ** -0.5
RING = 4
TURN_LAG, PV_LAG = 3, 7
QUAD = 4
CHUNKS = 4


ONE = 1


class Awaited:

    def __init__(self, eng, sem, a_turn, start=0):
        self.eng, self.sem, self.a_turn, self.start, self.base = eng, sem, a_turn, start, None

    def enter_loop(self):
        self.base = self.eng.alloc_register(f"{self.sem.name}_base_{self.eng.engine.name}")
        self.value = self.eng.alloc_register(f"{self.sem.name}_value_{self.eng.engine.name}")
        self.eng.reg_mov(self.base, self.start)

    def wait_ge(self, more):
        if self.base is None:
            self.eng.wait_ge(self.sem, self.start + more)
        elif more == 0:
            self.eng.wait_ge(self.sem, self.base)
        else:
            self.eng.reg_add(self.value, self.base, more)
            self.eng.wait_ge(self.sem, self.value)

    def next_turn(self):
        if self.base is None:
            self.start += self.a_turn
        else:
            self.eng.reg_add(self.base, self.base, self.a_turn)


def attention_stage(nc, q_dram, k_dram, ek_dram, rx_dram, rel_dram, rv_dram, v_parts, ident, o_all, sums):
    with ExitStack() as ctx:
        def sb(name, shape, dt=F32):
            return ctx.enter_context(nc.sbuf_tensor(name, shape, dt))

        def sem(name):
            return ctx.enter_context(nc.semaphore(name))

        k_st = sb("k_st", [STACK, GROUPS, HEADS, BG, S], BF16)
        q_st = [sb(f"q_st{i}", [STACK, HEADS, BG, WQ], BF16) for i in range(2)]
        e_st = [sb(f"e_st{i}", [STACK, EXTW], BF16) for i in range(2)]
        rpv = sb("rpv", [P, KC, WQ, NPART, HD], BF16)
        pt_hi = sb("pt_hi", [P, KC, NB * WQ], F16)
        pt_lo = sb("pt_lo", [P, KC, NB * WQ], F16)
        rel_out = sb("rel_out", [P, 2, 2, 2 * S])
        rel_in = sb("rel_in", [P, SLOTS, QUAD, S])
        scores = sb("scores", [P, RING, S])
        probs = sb("probs", [P, RING, S])
        low = sb("low", [P, 2, TILES])
        rv = sb("rv", [P, PAIRS, HD])
        idle_p = sb("idle_p", [1, 2])
        idle = sb("idle", [1, TILES // 2])
        ps_rel = ctx.enter_context(nc.psum_tensor("ps_rel", [P, 2, 512], F32))
        ps_sc = ctx.enter_context(nc.psum_tensor("ps_sc", [P, 4, S], F32))
        ps_pt = ctx.enter_context(nc.psum_tensor("ps_pt", [P, 2, 2, KC, P], F32))
        ps_o = ctx.enter_context(nc.psum_tensor("ps_o", [P, 2, 512], F32))

        k_loaded = [sem(f"k_loaded{b}") for b in range(GROUPS)]
        q_loaded = [sem(f"q_loaded{i}") for i in range(2)]
        rpv_loaded = sem("rpv_loaded")
        rel_made = sem("rel_made")
        rel_copied = sem("rel_copied")
        rel_sent = [[sem(f"rel_sent{i}{j}") for j in range(2)] for i in range(2)]
        rel_back = [sem(f"rel_back{i}") for i in range(SLOTS)]
        content_done = sem("content_done")
        added = sem("added")
        exp_done = sem("exp_done2")
        turned = sem("turned2")
        hi_done = sem("hi_done")
        lo_done = sem("lo_done")
        acc_made = sem("acc_made")
        acc_out = sem("acc_out")
        rv_sent = sem("rv_sent")
        idle_set = sem("idle_set")
        rv_free = sem("rv_free")
        START = SLOTS * QUAD
        SENT = 4 * 32
        QUADS = TILES // QUAD
        ACCS = QUADS + CHUNKS

        block = ctx.enter_context(nc.Block())

        def load_window(eng, w, g):
            for t in range(len(Q_TERMS)):
                eng.dma_start(q_st[g][t * HD:(t + 1) * HD, :, :, :].rearrange("d h b q -> d h (b q)"),
                              q_dram[bass.ds(w + g * NWIN, 1), Q_TERMS[t], :, :, :].rearrange(
                                  "n (h d) b q -> d (n h) (b q)", d=HD)).then_inc(q_loaded[g], 16)
            eng.dma_start(e_st[g][:, :], ek_dram[:, bass.ds((NWIN - 1 - w) * WQ, EXTW)]).then_inc(q_loaded[g], 16)

        LOADS = 16 * (len(Q_TERMS) + 1)

        @block.gpsimd
        def _(pool):
            pool.memset(idle_p[:, 0:1], 0.0).then_inc(idle_set, 1)
            for g in range(GROUPS):
                load_window(pool, 0, g)
            pool.wait_ge(idle_set, 1)
            with pool.Fori(0, NWIN) as w:
                for g in range(GROUPS):
                    n = GROUPS * w + g
                    if g == 0:
                        pool.wait_ge(acc_made, ACCS * n + ONE)
                        pool.wait_ge(q_loaded[0], LOADS)
                        for c in range(KC):
                            pool.dma_start(rpv[:, c, :, :, :].rearrange("p q a d -> p (q a d)"),
                                           rx_dram[bass.ds(w, 1), c, :, :].rearrange("w p x -> p (w x)")
                                           ).then_inc(rpv_loaded, 16)
                    pool.wait_ge(content_done, TILES * (n + 1))
                    pool.wait_ge(q_loaded[0], LOADS)
                    load_window(pool, (w + 1) % NWIN, g)
                    pool.wait_ge(acc_out, ACCS * (n + 1) + ONE)
                    pool.wait_ge(q_loaded[0], LOADS)
                    for half in range(2):
                        pool.dma_start(rv_dram[bass.ds(n, 1), :, half, :].rearrange("n r x -> (n r) x"),
                                       rv[half * NB:(half + 1) * NB, :, :].rearrange("r q d -> r (q d)")).then_inc(rv_sent, 16)
                    pool.wait_ge(rv_sent, 32 * (n + 1))
                    pool.tensor_tensor(idle_p[:, 1:2], idle_p[:, 0:1], idle_p[:, 0:1], ALU.add).then_inc(rv_free, 1)
            for g in range(GROUPS):
                pool.wait_ge(q_loaded[g], LOADS * (NWIN + 1))

        @block.sync
        def _(sp):
            for g in range(GROUPS):
                for t in range(len(K_TERMS)):
                    sp.dma_start(k_st[t * HD:(t + 1) * HD, g, :, :, :].rearrange("d h b k -> d h (b k)"),
                                 k_dram[K_TERMS[t], :, g * BG:(g + 1) * BG, :].rearrange("(h d) b k -> d h (b k)", d=HD)
                                 ).then_inc(k_loaded[g], 16)

            def send(g, base, j):
                sp.wait_ge(rel_copied, base + 2 * (j + 1))
                for half in range(2):
                    sp.dma_start(rel_dram[g, :, half, 4 * j * S:4 * (j + 1) * S],
                                 rel_out[half * NB:(half + 1) * NB, j % 2, :, :].rearrange("r a b -> r (a b)")
                                 ).then_inc(rel_sent[g][j % 2], 16)

            for j in range(QUADS):
                send(0, 0, j)
            with sp.Fori(0, NWIN) as w:
                for g in range(GROUPS):
                    n = GROUPS * w + g
                    for slot in range(2):
                        sp.wait_ge(rel_sent[g][slot], SENT * (w + 1))
                    rows = rel_dram[g, :, :, :].rearrange("(t u) v (q k) -> (u v q) t k", u=2, k=S)

                    def bring(j):
                        sp.wait_ge(added, TILES * n + QUAD * (j + 1))
                        sp.dma_start(rel_in[:, j % SLOTS, :, :], rows[:, QUAD * j:QUAD * (j + 1), :]
                                     ).then_inc(rel_back[j % SLOTS], 16)

                    for j in range(SLOTS):
                        bring(j)
                    for j in range(QUADS):
                        send(1 - g, TILES // 2 * (n + 1), j)
                        if j + SLOTS < QUADS:
                            bring(j + SLOTS)
            for slot in range(2):
                sp.wait_ge(rel_sent[0][slot], SENT * (NWIN + 1))

        @block.tensor
        def _(pe):
            def relative(i, m):
                for half in range(2):
                    q = m + half * PAIRS
                    ins = pe.matmul(ps_rel[half * NB:(half + 1) * NB, m // 2 % 2, (m % 2) * S:(m % 2 + 1) * S],
                                    q_st[i][:, :, :, q].rearrange("s h b -> s (h b)"),
                                    e_st[i][:, WQ - 1 - q:WQ - 1 - q + S], start=True, stop=True)
                if m % 2:
                    ins.then_inc(rel_made, 1)

            pe.wait_ge(q_loaded[0], LOADS)
            for m in range(PAIRS):
                if m >= 4 and m % 2 == 0:
                    pe.wait_ge(rel_copied, m // 2 - 1)
                relative(0, m)
            added_, exp_, lo_ = (Awaited(pe, sem, per, start) for sem, per, start in (
                (added, TILES, START), (exp_done, TILES, RING - 1), (lo_done, TILES // 2, ONE)))
            copied_, out_ = Awaited(pe, rel_copied, TILES // 2, TILES // 2), Awaited(pe, acc_out, ACCS, ONE)
            for awaited in (added_, exp_, lo_, copied_, out_):
                awaited.enter_loop()
            with pe.Fori(0, NWIN) as w:
                for g in range(GROUPS):
                    n = GROUPS * w + g

                    def content(t):
                        h, b = t // 2, 2 * (t % 2)
                        if t % 2 == 0:
                            added_.wait_ge(t - 2)
                        for u in range(2):
                            ins = pe.matmul(ps_sc[u * WQ:(u + 1) * WQ, t % 4, :], q_st[g][:, h, b + u, :],
                                            k_st[:, g, h, b + u, :], start=True, stop=True)
                        ins.then_inc(content_done, 1)

                    def turn(t):
                        exp_.wait_ge(t + 1)
                        if t % 2 == 0:
                            lo_.wait_ge(max(t // 2 - 1, 0))
                        for c in range(KC):
                            ins = pe.transpose(ps_pt[:, t // 2 % 2, t % 2, c, :], probs[:, t % RING, c * P:(c + 1) * P],
                                               ident[:, :])
                        ins.then_inc(turned, 1)

                    def values(t):
                        a = t // QUAD
                        if t % 2 == 0:
                            lo_.wait_ge(t // 2 + 1)
                        if t % QUAD == 0:
                            out_.wait_ge(max(a - 1, 0))
                        h, b = t // 2, 2 * (t % 2)
                        out = ps_o[:, a % 2, (t % QUAD) * 96:(t % QUAD) * 96 + 96].rearrange("p (a u d) -> p a u d", a=NPART, u=2)
                        for pt, parts in ((pt_hi, 3), (pt_lo, 2)):
                            for c in range(KC):
                                ins = pe.matmul(out[:, 0:parts, :, :], pt[:, c, t * P:(t + 1) * P],
                                                v_parts[:, 0:parts, c, g * BG + b:g * BG + b + 2,
                                                        h * HD:(h + 1) * HD],
                                                start=(parts == 3 and c == 0), stop=(parts == 2 and c == KC - 1))
                        if t % QUAD == QUAD - 1:
                            ins.then_inc(acc_made, 1)

                    for s in range(TILES + PV_LAG):
                        if s < TILES:
                            if s == 0:
                                pe.wait_ge(k_loaded[g], 16 * len(K_TERMS))
                                pe.wait_ge(q_loaded[1 - g], LOADS * (w + 1 + g))
                            content(s)
                            if s % 2 == 0:
                                copied_.wait_ge(s // 2 - 1)
                            relative(1 - g, s)
                        if 0 <= s - TURN_LAG < TILES:
                            turn(s - TURN_LAG)
                        if 0 <= s - PV_LAG < TILES:
                            values(s - PV_LAG)
                    pe.wait_ge(rpv_loaded, 16 * KC * (w + 1))
                    for m in range(PAIRS):
                        a = TILES // QUAD + m // 8
                        if m % 8 == 0:
                            out_.wait_ge(a - 1)
                        for pt, parts in ((pt_hi, 3), (pt_lo, 2)):
                            for c in range(KC):
                                for half in range(2):
                                    q = m + half * PAIRS
                                    cols = (m % 8) * 48
                                    ins = pe.matmul(
                                        ps_o[half * NB:(half + 1) * NB, a % 2, cols:cols + parts * HD],
                                        pt[:, c, q:NB * WQ:WQ], rpv[:, c, WQ - 1 - q, 0:parts, :].rearrange("p a d -> p (a d)"),
                                        start=(parts == 3 and c == 0), stop=(parts == 2 and c == KC - 1))
                        if m % 8 == 7:
                            ins.then_inc(acc_made, 1)
                    for awaited in (added_, exp_, lo_, copied_, out_):
                        awaited.next_turn()

        @block.scalar
        def _(act):
            def relative_out(j):
                act.activation(rel_out[:, j // 2 % 2, j % 2, :], ps_rel[:, j % 2, :], ACT.Copy).then_inc(rel_copied, 1)

            for j in range(PAIRS // 2):
                if j >= 4 and j % 2 == 0:
                    act.wait_ge(rel_sent[0][j // 2 % 2], 32 * (j // 4))
                act.wait_ge(rel_made, j + 1)
                relative_out(j)
            added_, turned_ = Awaited(act, added, TILES, START), Awaited(act, turned, TILES, ONE)
            made_ = Awaited(act, rel_made, TILES // 2, TILES // 2)
            for awaited in (added_, turned_, made_):
                awaited.enter_loop()
            with act.Fori(0, NWIN) as w:
                for g in range(GROUPS):
                    n = GROUPS * w + g
                    for s in range(TILES + TURN_LAG + 2):
                        if s < TILES:
                            t = s
                            added_.wait_ge(t + 1)
                            turned_.wait_ge(max(t - RING + 1, 0))
                            act.activation(probs[:, t % RING, :], scores[:, t % RING, :], ACT.Exp, scale=-1.0,
                                           bias=low[:, g, t:t + 1],
                                           accum_out=sums[:, bass.ds(n, 1), t:t + 1].rearrange("p o t -> p (o t)")
                                           ).then_inc(exp_done, 1)
                            if s % 2:
                                j = s // 2
                                if j % 2 == 0:
                                    if j >= 4:
                                        act.wait_ge(rel_sent[1 - g][j // 2 % 2], SENT * (w + g) + 32 * (j // 4))
                                    else:
                                        act.wait_ge(rel_sent[g][j // 2 % 2], SENT * (w + 1))
                                made_.wait_ge(j + 1)
                                relative_out(j)
                        t = s - TURN_LAG - 1
                        if 0 <= t < TILES and t % 2:
                            turned_.wait_ge(t + 1)
                            if t == 1:
                                act.wait_ge(acc_made, ACCS * n + ONE)
                            act.activation(pt_hi[:, :, (t - 1) * P:(t + 1) * P].rearrange("p c (t x) -> p t c x", t=2),
                                           ps_pt[:, t // 2 % 2, :, :, :], ACT.Copy).then_inc(hi_done, 1)
                    for awaited in (added_, turned_, made_):
                        awaited.next_turn()

        @block.vector
        def _(dve):
            dve.engine_nop().then_inc(added, START)
            dve.engine_nop().then_inc(exp_done, RING - 1)
            for counts in (lo_done, acc_out, turned, acc_made, rv_free):
                dve.engine_nop().then_inc(counts, ONE)
            content_, exp_ = Awaited(dve, content_done, TILES), Awaited(dve, exp_done, TILES, RING - 1)
            hi_, made_ = Awaited(dve, hi_done, TILES // 2), Awaited(dve, acc_made, ACCS, ONE)
            for awaited in (content_, exp_, hi_, made_):
                awaited.enter_loop()
            with dve.Fori(0, NWIN) as w:
                for g in range(GROUPS):
                    n = GROUPS * w + g
                    for s in range(TILES + PV_LAG + 2):
                        if s < TILES:
                            t = s
                            if t % QUAD == 0:
                                j = t // QUAD
                                dve.wait_ge(rel_back[j % SLOTS], 16 * (TILES // QUAD // SLOTS * n + j // SLOTS + 1))
                            if t % 2 == 0:
                                content_.wait_ge(t + 2)
                                exp_.wait_ge(t - RING + 2)
                                dve.memset(idle[:, t // 2:t // 2 + 1], 0.0)
                            ins = dve.tensor_tensor_reduce(scores[:, t % RING, :], ps_sc[:, t % 4, :],
                                                           rel_in[:, t // QUAD % SLOTS, t % QUAD, :], -SCALE, 3.0e38,
                                                           ALU.add, ALU.min, low[:, g, t:t + 1])
                            ins.then_inc(added, 1)
                        t = s - TURN_LAG - 1
                        if 0 <= t < TILES and t % 2:
                            hi_.wait_ge(t // 2 + 1)
                            cols = slice((t - 1) * P, (t + 1) * P)
                            dve.tensor_tensor(pt_lo[:, :, cols].rearrange("p c (t x) -> p t c x", t=2),
                                              ps_pt[:, t // 2 % 2, :, :, :],
                                              pt_hi[:, :, cols].rearrange("p c (t x) -> p t c x", t=2),
                                              ALU.subtract).then_inc(lo_done, 1)
                        t = s - PV_LAG - 1
                        if 0 <= t < TILES and t % QUAD == QUAD - 1:
                            a = t // QUAD
                            made_.wait_ge(a + 1)
                            acc = ps_o[:, a % 2, 0:QUAD * 96].rearrange("p (t a d) -> p t d a", t=QUAD, a=NPART)
                            for u in range(2):
                                rows = slice(u * WQ, (u + 1) * WQ)
                                ins = dve.tensor_reduce(
                                    o_all[rows, bass.ds(n, 1), QUAD * a:QUAD * (a + 1), :].rearrange("p o t d -> p (o t) d"),
                                    acc[rows, :, u * HD:(u + 1) * HD, :], AX.X, ALU.add)
                            ins.then_inc(acc_out, 1)
                    for c in range(CHUNKS):
                        a = TILES // QUAD + c
                        made_.wait_ge(a + 1)
                        if c == 0:
                            dve.wait_ge(rv_free, n + ONE)
                        dve.tensor_reduce(rv[:, 8 * c:8 * c + 8, :],
                                          ps_o[:, a % 2, 0:8 * 48].rearrange("p (q a d) -> p q d a", q=8, a=NPART),
                                          AX.X, ALU.add).then_inc(acc_out, 1)
                    for awaited in (content_, exp_, hi_, made_):
                        awaited.next_turn()


BLOCKS = TOK // P + EXPERTS - 1
WSLOTS = 4
LN_GROUP = 4
HALVES = 2
HH = HID // HALVES
HC = HH // P
B1 = EXPERTS * 2 * HID // P
B2 = EXPERTS * D // P


def feed_forward_stage(nc, h_dram, rv_dram, o_all, sums, ident, wo_t, bo, router_w, router_b, w1, b1, w2, b2,
                       b1p_dram, b2p_dram, xs_dram, ys_dram, out):
    with ExitStack() as ctx:
        def sb(name, shape, dt=F32):
            return ctx.enter_context(nc.sbuf_tensor(name, shape, dt))

        def sem(name):
            return ctx.enter_context(nc.semaphore(name))

        h2 = sb("h2", [P, TT, D])
        xs = sb("xs", [P, BLOCKS, D])
        xn2 = xs[:, 0:TT, :]
        early = sb("early", [P, WINDOWS * TILES * HD])
        rv_in = early[:, :].rearrange("p (n t d) -> p n t d", n=WINDOWS, d=HD)
        eg, u = (early[:, i * HID:(i + 1) * HID].rearrange("p (a n) -> p a n", a=HALVES) for i in range(2))
        ut = early[:, 2 * HID:3 * HID].rearrange("p (a c n) -> p a c n", a=HALVES, n=P)
        xst = early[:, 3 * HID:3 * HID + D].rearrange("p (c n) -> p c n", c=KC)
        rec = sb("rec", [P, WINDOWS, TILES])
        osum = sb("osum", [P, 2, TILES, HD])
        attn = sb("attn", [P, 2, 2, D])
        attn_t = sb("attn_t", [P, 2, KC, P])
        wo = sb("wo", [P, KC, D])
        bo_b = sb("bo_b", [P, D])
        rw = sb("rw", [P, KC, EXPERTS])
        rb = sb("rb", [P, EXPERTS])
        stats2 = sb("stats2", [P, TT, 6])
        mv2 = sb("mv2", [P, TT, 2])
        var2 = sb("var2", [P, TT])
        sd2 = sb("sd2", [P, TT])
        rs2 = sb("rs2", [P, 4, TT])
        xn2t = sb("xn2t", [P, 2, KC, P])
        bias = sb("bias", [P, B1 + B2])
        bias3 = sb("bias3", [P, NPART, B1 + B2], BF16)
        b1s = sb("b1s", [NPART * EXPERTS, 2 * HID], BF16)
        b2s = sb("b2s", [NPART * EXPERTS, D], BF16)
        pick_f = osum[0:NPART * EXPERTS, :, :, :].rearrange("r a t d -> r (a t d)").rearrange("r (e n) -> r e n", n=P)
        pick = sb("pick", [NPART * EXPERTS, EXPERTS, P], BF16)
        below = sb("below", [P, P])
        ones = sb("ones", [P, P])
        ints = sb("ints", [P, EXPERTS + TT * EXPERTS + BLOCKS], I32)
        floats = sb("floats", [P, EXPERTS + TT * EXPERTS + BLOCKS])
        route = sb("route", [P, 6, TT, EXPERTS])
        best = sb("best", [P, 2, TT])
        past = sb("past", [P, 6, EXPERTS])
        over = sb("over", [P, EXPERTS, TT])
        slot_f = sb("slot_f", [P, TT])
        slot = sb("slot", [P, TT], U32)
        later = sb("later", [P, BLOCKS, EXPERTS - 1])
        block_f = sb("block_f", [P, 4, BLOCKS])
        block_i = sb("block_i", [P, 2, BLOCKS], I32)
        start_i = sb("start_i", [P, EXPERTS], I32)
        x_now = sb("x_now", [P, D])
        w1s = sb("w1s", [P, WSLOTS, KC, 2 * HID])
        w2s = sb("w2s", [P, WSLOTS, HID // P, D])
        psum = ctx.enter_context(nc.psum_tensor("psum3", [P, 8, 512], F32))

        weights_in = sem("weights_in")
        rv_back = [sem(f"rv_back{n}") for n in range(WINDOWS)]
        h_back = sem("h_back")
        made = sem("made")
        bias_added = sem("bias_added")
        zeroed = sem("zeroed")
        step = sem("step")
        attn_ready = sem("attn_ready")
        attn_turned = sem("attn_turned")
        attn_out = sem("attn_out")
        o_made = sem("o_made")
        h_added = sem("h_added")
        var2_ready = sem("var2_ready")
        sd2_done = sem("sd2_done")
        normed = sem("normed")
        xn_turned = sem("xn_turned")
        xn_out = sem("xn_out")
        logits_done = sem("logits_done")
        chosen = sem("chosen")
        counted = sem("counted")
        slots_ready = sem("slots_ready")
        bias_split = sem("bias_split")
        bias_sent = sem("bias_sent")
        bias_back = sem("bias_back")
        scattered = sem("scattered")
        xs_in = sem("xs_in")
        w_slot = [sem(f"w_slot{i}") for i in range(WSLOTS)]
        experts_in = sem("experts_in")
        x_picked = sem("x_picked")
        xs_turned = sem("xs_turned")
        xs_out = sem("xs_out")
        h_made = sem("h_made")
        exp3_done = sem("exp3_done")
        gate_step = sem("gate_step")
        gated = sem("gated")
        u_turned = sem("u_turned")
        u_out = sem("u_out")
        y_made = sem("y_made")
        y_out = sem("y_out")
        y_sent = sem("y_sent")
        y_back = [sem(f"y_back{i}") for i in range(4)]
        final = sem("final")
        out_sent = sem("out_sent")

        yg = xn2
        iota8, thresh, block_no = (floats[:, 0:EXPERTS], floats[:, EXPERTS:EXPERTS * (TT + 1)],
                                   floats[:, EXPERTS * (TT + 1):])

        def rows_of(dram, w, half):
            return dram.rearrange("(m u w q) c -> u w q m c", u=2, w=NWIN, q=WQ)[half, w]

        def tiles_of(sbuf, w, half):
            return sbuf.rearrange("p (w m) c -> p w m c", w=NWIN)[half * WQ:(half + 1) * WQ, w]

        block = ctx.enter_context(nc.Block())

        @block.sync
        def _(sp):
            def load_expert(e):
                sp.dma_start(w1s[:, e % WSLOTS, :, :], w1[e].rearrange("(k p) n -> p k n", p=P)
                             ).then_inc(w_slot[e % WSLOTS], 16)
                sp.dma_start(w2s[:, e % WSLOTS, :, :], w2[e].rearrange("(k p) n -> p k n", p=P)
                             ).then_inc(w_slot[e % WSLOTS], 16)

            for n in range(WINDOWS):
                sp.dma_start(rv_in[:, n, :, :], rv_dram[n].rearrange("(t u) v (q d) -> (u v q) t d", u=2, d=HD)
                             ).then_inc(rv_back[n], 16)
            sp.dma_start(wo[:, :, :], wo_t.rearrange("(k p) n -> p k n", p=P)).then_inc(weights_in, 16)
            sp.dma_start(bo_b[:, :], bo.rearrange("(a n) -> a n", a=1).broadcast_to([P, D])).then_inc(weights_in, 16)
            sp.dma_start(rw[:, :, :], router_w.rearrange("(k p) n -> p k n", p=P)).then_inc(weights_in, 16)
            sp.dma_start(rb[:, :], router_b.rearrange("(a n) -> a n", a=1).broadcast_to([P, EXPERTS])
                         ).then_inc(weights_in, 16)
            sp.dma_start(bias[:, 0:B1], b1.rearrange("e (a n) -> (e a) n", n=B1)).then_inc(weights_in, 16)
            sp.dma_start(bias[:, B1:], b2.rearrange("e (a n) -> (e a) n", n=B2)).then_inc(weights_in, 16)
            for e in range(WSLOTS):
                load_expert(e)
            sp.wait_ge(bias_split, 1)
            for a in range(NPART):
                sp.dma_start(b1p_dram[a].rearrange("(p n) -> p n", p=P), bias3[:, a, 0:B1]).then_inc(bias_sent, 16)
                sp.dma_start(b2p_dram[a].rearrange("(p n) -> p n", p=P), bias3[:, a, B1:]).then_inc(bias_sent, 16)
            sp.wait_ge(bias_sent, 16 * 2 * NPART)
            sp.dma_start(b1s[:, :], b1p_dram.rearrange("a (e n) -> (a e) n", e=EXPERTS)).then_inc(bias_back, 16)
            sp.dma_start(b2s[:, :], b2p_dram.rearrange("a (e n) -> (a e) n", e=EXPERTS)).then_inc(bias_back, 16)
            sp.wait_ge(scattered, 16 * TT)
            sp.dma_start(xs[:, :, :], xs_dram.rearrange("(k p) c -> p k c", p=P)).then_inc(xs_in, 16)
            sp.wait_ge(slots_ready, 1)
            for e in range(WSLOTS, EXPERTS):
                sp.wait_ge(y_made, sp.value_load(start_i[0:1, e - WSLOTS + 1:e - WSLOTS + 2], min_val=1, max_val=BLOCKS))
                load_expert(e)
            for w in range(NWIN):
                sp.wait_ge(final, 4 * (w + 1))
                for half in range(2):
                    sp.dma_start(rows_of(out, w, half), tiles_of(h2, w, half)).then_inc(out_sent, 16)
            sp.wait_ge(out_sent, 16 * 2 * NWIN)

        @block.gpsimd
        def _(pool):
            pool.memset(xs[:, :, :], 0.0).then_inc(made, 1)
            pool.memset(ones[:, :], 1.0).then_inc(made, 1)
            pool.memset(pick_f[:, :, :], 0.0).then_inc(made, 1)
            pool.iota(ints[:, 0:EXPERTS], pattern=[[1, EXPERTS]], base=0, channel_multiplier=0).then_inc(made, 1)
            pool.iota(ints[:, EXPERTS:EXPERTS * (TT + 1)], pattern=[[0, EXPERTS], [P, TT]], base=0,
                      channel_multiplier=0).then_inc(made, 1)
            pool.iota(ints[:, EXPERTS * (TT + 1):], pattern=[[1, BLOCKS]], base=0, channel_multiplier=0).then_inc(made, 1)
            pool.wait_ge(made, 6)
            pool.dma_start(xs_dram.rearrange("(k p) c -> p k c", p=P), xs[:, :, :]).then_inc(zeroed, 16)
            pool.affine_select(out=below[:, :], in_=ones[:, :], compare_op=ALU.is_ge, fill=0.0, base=-1,
                               pattern=[[1, P]], channel_multiplier=-1).then_inc(made, 1)
            for a in range(NPART):
                pool.affine_select(out=pick_f[:, :, :], in_=pick_f[:, :, :], compare_op=ALU.not_equal, fill=1.0,
                                   base=-EXPERTS * a, pattern=[[-1, EXPERTS], [0, P]],
                                   channel_multiplier=1).then_inc(made, 1)
                pool.wait_ge(made, 8 + a)
            pool.wait_ge(weights_in, 16 * 6)
            pool.wait_ge(h_back, 16 * 2 * NWIN)
            for i in range(TT):
                pool.tensor_tensor(h2[:, i, :], h2[:, i, :], bo_b[:, :], ALU.add).then_inc(bias_added, 1)
            pool.wait_ge(zeroed, 16)
            pool.wait_ge(slots_ready, 1)
            for i in range(TT):
                pool.indirect_dma_start(xs_dram, bass.IndirectOffsetOnAxis(slot[:, i:i + 1], 0), xn2[:, i, :],
                                        None).then_inc(scattered, 16)
            for e in range(EXPERTS):
                pool.wait_ge(w_slot[e % WSLOTS], 32 * (e // WSLOTS + 1))
                pool.engine_nop().then_inc(experts_in, 1)
            pool.wait_ge(scattered, 16 * TT)
            pool.wait_ge(y_sent, 16 * BLOCKS)
            for i in range(TT):
                pool.indirect_dma_start(yg[:, i, :], None, ys_dram, bass.IndirectOffsetOnAxis(slot[:, i:i + 1], 0)
                                        ).then_inc(y_back[i // 4], 16)

        @block.tensor
        def _(pe):
            pe.wait_ge(weights_in, 16 * 6)
            for n in range(WINDOWS + 1):
                if n < WINDOWS:
                    pe.wait_ge(attn_ready, n + 1)
                    for bp in range(2):
                        i = 2 * n + bp
                        if i >= 2:
                            pe.wait_ge(attn_out, i - 1)
                        for c in range(KC):
                            ins = pe.transpose(psum[:, i % 2, c * P:(c + 1) * P], attn[:, n % 2, bp, c * P:(c + 1) * P],
                                               ident[:, :])
                        ins.then_inc(attn_turned, 1)
                    for bp in range(2):
                        i = 2 * n + bp
                        pe.wait_ge(attn_out, i + 1)
                        if i >= 2:
                            pe.wait_ge(h_added, i - 1)
                        for c in range(KC):
                            ins = pe.matmul(psum[:, 2 + i % 2, 0:D], attn_t[:, i % 2, c, :], wo[:, c, :],
                                            start=(c == 0), stop=(c == KC - 1))
                        ins.then_inc(o_made, 1)
                if n >= 2 and n % 2 == 0:
                    for i in range(2 * n - LN_GROUP, 2 * n):
                        pe.wait_ge(normed, i + 1)
                        if i >= 2:
                            pe.wait_ge(xn_out, i - 1)
                        for c in range(KC):
                            ins = pe.transpose(psum[:, 4 + i % 2, c * P:(c + 1) * P], xn2[:, i, c * P:(c + 1) * P],
                                               ident[:, :])
                        ins.then_inc(xn_turned, 1)
                        pe.wait_ge(xn_out, i + 1)
                        for c in range(KC):
                            ins = pe.matmul(psum[:, 6, i * EXPERTS:(i + 1) * EXPERTS], xn2t[:, i % 2, c, :], rw[:, c, :],
                                            start=(c == 0), stop=(c == KC - 1))
                        ins.then_inc(logits_done, 1)
            pe.wait_ge(made, 7)
            pe.wait_ge(chosen, 1)
            hot = route[:, 2, :, :].rearrange("p t e -> p (t e)")
            pe.matmul(psum[:, 7, 0:P], below[:, :], hot, start=True, stop=True)
            pe.matmul(psum[:, 7, P:2 * P], ones[:, :], hot, start=True, stop=True).then_inc(counted, 1)

            pe.wait_ge(bias_back, 32)
            pe.wait_ge(slots_ready, 1)

            def turn_tokens(ahead):
                x_picked_.wait_ge(ahead + 1)
                for c in range(KC):
                    ins = pe.transpose(psum[:, 7, c * P:(c + 1) * P], x_now[:, c * P:(c + 1) * P], ident[:, :])
                ins.then_inc(xs_turned, 1)

            def hidden(e, ws, half):
                for part in range(2):
                    cols = part * HID + half * HH
                    bank = 2 * half + part
                    pe.matmul(psum[:, bank, :], pick[:, bass.ds(e, 1), :].rearrange("r o p -> r (o p)"),
                              b1s[:, cols:cols + HH], start=True, stop=False)
                    for c in range(KC):
                        ins = pe.matmul(psum[:, bank, :], xst[:, c, :],
                                        w1s[:, bass.ds(ws, 1), c, cols:cols + HH].rearrange("p o n -> p (o n)"),
                                        start=False, stop=(c == KC - 1))
                ins.then_inc(h_made, 1)

            def turn_units(half):
                for c in range(HC):
                    ins = pe.transpose(psum[:, 4 + half, c * P:(c + 1) * P], u[:, half, c * P:(c + 1) * P], ident[:, :])
                ins.then_inc(u_turned, 1)

            def output(e, ws, half):
                if half == 0:
                    pe.matmul(psum[:, 6, 0:D], pick[:, bass.ds(e, 1), :].rearrange("r o p -> r (o p)"), b2s[:, :],
                              start=True, stop=False)
                for c in range(HC):
                    ins = pe.matmul(psum[:, 6, 0:D], ut[:, half, c, :],
                                    w2s[:, bass.ds(ws, 1), half * HC + c, :].rearrange("p o n -> p (o n)"),
                                    start=False, stop=(half == 1 and c == HC - 1))
                if half:
                    ins.then_inc(y_made, 1)

            xs_out_, gated_ = Awaited(pe, xs_out, 1), Awaited(pe, gated, HALVES)
            u_out_, y_out_ = Awaited(pe, u_out, HALVES), Awaited(pe, y_out, 1, ONE)
            x_picked_ = Awaited(pe, x_picked, 1)
            awaited_all = (xs_out_, gated_, u_out_, y_out_, x_picked_)

            def expert_of(k):
                return (pe.value_load(block_i[0:1, 0, bass.ds(k, 1)], min_val=0, max_val=EXPERTS - 1),
                        pe.value_load(block_i[0:1, 1, bass.ds(k, 1)], min_val=0, max_val=WSLOTS - 1))

            def finish(e, ws, between):
                gated_.wait_ge(0)
                turn_units(1)
                u_out_.wait_ge(-1)
                y_out_.wait_ge(-1)
                output(e, ws, 0)
                between()
                u_out_.wait_ge(0)
                output(e, ws, 1)

            def block_steps(k, first=False, last=False):
                e, ws = expert_of(k)
                pe.wait_ge(experts_in, e + 1)
                xs_out_.wait_ge(1)
                hidden(e, ws, 0)

                def second_half():
                    hidden(e, ws, 1)
                    if not last:
                        turn_tokens(1)
                    gated_.wait_ge(1)
                    turn_units(0)

                if first:
                    second_half()
                else:
                    finish(*expert_of(k - 1), second_half)
                for awaited in awaited_all:
                    awaited.next_turn()

            turn_tokens(0)
            block_steps(0, first=True)
            for awaited in awaited_all:
                awaited.enter_loop()
            with pe.Fori(1, BLOCKS - 1) as k:
                block_steps(k)
            block_steps(BLOCKS - 1, last=True)
            finish(*expert_of(BLOCKS - 1), lambda: None)

        @block.scalar
        def _(act):
            for w in range(NWIN):
                for half in range(2):
                    act.dma_start(tiles_of(h2, w, half), rows_of(h_dram, w, half)).then_inc(h_back, 16)
            for n in range(WINDOWS + 1):
                if n < WINDOWS:
                    for bp in range(2):
                        i = 2 * n + bp
                        act.wait_ge(attn_turned, i + 1)
                        if i >= 2:
                            act.wait_ge(o_made, i - 1)
                        act.activation(attn_t[:, i % 2, :, :], psum[:, i % 2, 0:D].rearrange("p (c n) -> p c n", c=KC),
                                       ACT.Copy).then_inc(attn_out, 1)
                if n >= 2 and n % 2 == 0:
                    tiles = slice(2 * n - LN_GROUP, 2 * n)
                    act.wait_ge(var2_ready, n // 2)
                    act.activation(sd2[:, tiles], var2[:, tiles], ACT.Sqrt).then_inc(sd2_done, 1)
                    for i in range(2 * n - LN_GROUP, 2 * n):
                        act.wait_ge(xn_turned, i + 1)
                        if i >= 2:
                            act.wait_ge(logits_done, i - 1)
                        act.activation(xn2t[:, i % 2, :, :], psum[:, 4 + i % 2, 0:D].rearrange("p (c n) -> p c n", c=KC),
                                       ACT.Copy).then_inc(xn_out, 1)

            h_made_, u_turned_ = Awaited(act, h_made, HALVES), Awaited(act, u_turned, HALVES)
            xs_turned_, y_made_, y_out_ = Awaited(act, xs_turned, 1), Awaited(act, y_made, 1), Awaited(act, y_out, 1, ONE)
            awaited_all = (h_made_, u_turned_, xs_turned_, y_made_, y_out_)

            def exponents(half):
                h_made_.wait_ge(half + 1)
                act.activation(eg[:, half, :], psum[:, 2 * half + 1, :], ACT.Exp, scale=-1.0).then_inc(exp3_done, 1)

            def tokens_out():
                act.activation(xst[:, :, :], psum[:, 7, 0:D].rearrange("p (c n) -> p c n", c=KC), ACT.Copy
                               ).then_inc(xs_out, 1)

            def units_out(half):
                act.activation(ut[:, half, :, :], psum[:, 4 + half, :].rearrange("p (c n) -> p c n", c=HC), ACT.Copy
                               ).then_inc(u_out, 1)

            def outputs_out(k):
                y_made_.wait_ge(0)
                act.activation(xs[:, bass.ds(k, 1), :].rearrange("p o c -> p (o c)"), psum[:, 6, 0:D], ACT.Copy
                               ).then_inc(y_out, 1)
                y_out_.wait_ge(0)
                act.dma_start(ys_dram[bass.ds(k * P, P), :], xs[:, bass.ds(k, 1), :].rearrange("p o c -> p (o c)")
                              ).then_inc(y_sent, 16)

            def block_steps(k, first=False, last=False):
                exponents(0)
                if not first:
                    u_turned_.wait_ge(0)
                    units_out(1)
                exponents(1)
                if not last:
                    xs_turned_.wait_ge(2)
                    tokens_out()
                u_turned_.wait_ge(1)
                units_out(0)
                if not first:
                    outputs_out(k - 1)
                for awaited in awaited_all:
                    awaited.next_turn()

            xs_turned_.wait_ge(1)
            tokens_out()
            block_steps(0, first=True)
            for awaited in awaited_all:
                awaited.enter_loop()
            with act.Fori(1, BLOCKS - 1) as k:
                block_steps(k)
            block_steps(BLOCKS - 1, last=True)
            u_turned_.wait_ge(0)
            units_out(1)
            outputs_out(BLOCKS - 1)

        @block.vector
        def _(dve):
            n_steps = [0]
            dve.engine_nop().then_inc(y_out, ONE)

            def follow(ins):
                n_steps[0] += 1
                ins.then_inc(step, 1)
                dve.wait_ge(step, n_steps[0])

            def normalise(tiles):
                for i in tiles:
                    follow(dve.bn_stats(stats2[:, i, :], h2[:, i, :]))
                for i in tiles:
                    follow(dve.bn_aggr(mv2[:, i, :], stats2[:, i, :]))
                g = slice(tiles[0], tiles[-1] + 1)
                dve.tensor_scalar(var2[:, g], mv2[:, g, 1], EPS, None, ALU.add).then_inc(var2_ready, 1)
                dve.wait_ge(sd2_done, tiles[0] // LN_GROUP + 1)
                follow(dve.reciprocal(rs2[:, 0, g], sd2[:, g]))
                follow(dve.tensor_tensor(rs2[:, 1, g], rs2[:, 0, g], rs2[:, 0, g], ALU.mult))
                follow(dve.tensor_tensor(rs2[:, 2, g], rs2[:, 1, g], var2[:, g], ALU.mult))
                follow(dve.tensor_scalar(rs2[:, 1, g], rs2[:, 2, g], -0.5, 1.5, ALU.mult, ALU.add))
                follow(dve.tensor_tensor(rs2[:, 3, g], rs2[:, 0, g], rs2[:, 1, g], ALU.mult))
                for i in tiles:
                    dve.tensor_scalar(xn2[:, i, :], h2[:, i, :], mv2[:, i, 0:1], rs2[:, 3, i:i + 1],
                                      ALU.subtract, ALU.mult).then_inc(normed, 1)

            dve.wait_ge(made, 10)
            follow(dve.tensor_copy(pick[:, :, :], pick_f))
            follow(dve.reciprocal(rec[:, :, :], sums[:, :, :]))
            dve.wait_ge(weights_in, 16 * 6)
            for a in range(NPART):
                ins = dve.tensor_copy(bias3[:, a, :], bias[:, :])
                follow(ins)
                if a < NPART - 1:
                    follow(dve.tensor_tensor(bias[:, :], bias[:, :], bias3[:, a, :], ALU.subtract))
            dve.engine_nop().then_inc(bias_split, 1)
            for n in range(WINDOWS + 1):
                if n < WINDOWS:
                    dve.wait_ge(rv_back[n], 16)
                    follow(dve.tensor_tensor(osum[:, n % 2, :, :], o_all[:, n, :, :], rv_in[:, n, :, :], ALU.add))
                    if n >= 2:
                        dve.wait_ge(attn_turned, 2 * (n - 1))
                    dve.tensor_tensor(attn[:, n % 2, :, :].rearrange("p m (h d) -> p h m d", d=HD),
                                      osum[:, n % 2, :, :].rearrange("p (h m) d -> p h m d", m=2),
                                      rec[:, n, :].rearrange("p (h m) -> p h m", m=2).unsqueeze(3).broadcast_to(
                                          [P, HEADS, 2, HD]), ALU.mult).then_inc(attn_ready, 1)
                if n >= 1:
                    for i in (2 * n - 2, 2 * n - 1):
                        dve.wait_ge(o_made, i + 1)
                        dve.wait_ge(bias_added, i + 1)
                        dve.tensor_tensor(h2[:, i, :], psum[:, 2 + i % 2, 0:D], h2[:, i, :], ALU.add).then_inc(h_added, 1)
                if n >= 2 and n % 2 == 0:
                    dve.wait_ge(h_added, 2 * n)
                    dve.wait_ge(zeroed, 16)
                    normalise(range(2 * n - LN_GROUP, 2 * n))

            def per_tile(ap):
                return ap.unsqueeze(2).broadcast_to([P, TT, EXPERTS])

            def per_expert(ap):
                return ap.unsqueeze(1).broadcast_to([P, TT, EXPERTS])

            logits, cand, hot, acc_a, acc_b, rank = (route[:, i, :, :] for i in range(6))
            follow(dve.tensor_copy(floats[:, :], ints[:, :]))
            dve.wait_ge(logits_done, TT)
            follow(dve.tensor_tensor(logits, psum[:, 6, 0:TT * EXPERTS].rearrange("p (t e) -> p t e", e=EXPERTS),
                                     per_expert(rb[:, :]), ALU.add))
            follow(dve.tensor_reduce(best[:, 0, :], logits, AX.X, ALU.max))
            follow(dve.tensor_tensor(cand, logits, per_tile(best[:, 0, :]), ALU.is_equal))
            follow(dve.tensor_scalar(cand, cand, -100.0, None, ALU.mult))
            follow(dve.tensor_tensor(cand, cand, per_expert(iota8), ALU.add))
            follow(dve.tensor_reduce(best[:, 1, :], cand, AX.X, ALU.min))
            dve.tensor_tensor(hot, cand, per_tile(best[:, 1, :]), ALU.is_equal).then_inc(chosen, 1)
            dve.wait_ge(counted, 1)
            counts = psum[:, 7, P:2 * P].rearrange("p (t e) -> p t e", e=EXPERTS)
            follow(dve.tensor_copy(acc_a, counts))
            src, dst = acc_a, acc_b
            shift = 1
            while shift < TT:
                follow(dve.tensor_copy(dst[:, 0:shift, :], src[:, 0:shift, :]))
                follow(dve.tensor_tensor(dst[:, shift:, :], src[:, shift:, :], src[:, 0:TT - shift, :], ALU.add))
                src, dst = dst, src
                shift *= 2
            follow(dve.tensor_tensor(dst, src, counts, ALU.subtract))
            follow(dve.tensor_tensor(rank, psum[:, 7, 0:P].rearrange("p (t e) -> p t e", e=EXPERTS), dst, ALU.add))
            follow(dve.tensor_tensor(over[:, :, 0:TT - 1], src[:, TT - 1, :].unsqueeze(2).broadcast_to([P, EXPERTS, TT - 1]),
                                     thresh.rearrange("p (e t) -> p e t", e=EXPERTS)[:, :, 1:], ALU.is_gt))
            follow(dve.tensor_reduce(past[:, 1, :], over[:, :, 0:TT - 1], AX.X, ALU.add))
            follow(dve.tensor_scalar(past[:, 0, :], past[:, 1, :], 1.0, None, ALU.add))
            at, shift = 0, 1
            while shift < EXPERTS:
                follow(dve.tensor_copy(past[:, at + 1, 0:shift], past[:, at, 0:shift]))
                follow(dve.tensor_tensor(past[:, at + 1, shift:], past[:, at, shift:], past[:, at, 0:EXPERTS - shift],
                                         ALU.add))
                at, shift = at + 1, 2 * shift
            first = past[:, 4, :]
            follow(dve.tensor_tensor(first, past[:, at, :], past[:, 0, :], ALU.subtract))
            follow(dve.tensor_copy(start_i[:, :], first))
            follow(dve.tensor_scalar(past[:, 5, :], first, float(P), None, ALU.mult))
            follow(dve.tensor_tensor(rank, rank, per_expert(past[:, 5, :]), ALU.add))
            follow(dve.tensor_tensor(rank, rank, hot, ALU.mult))
            follow(dve.tensor_reduce(slot_f[:, :], rank, AX.X, ALU.add))
            follow(dve.tensor_copy(slot[:, :], slot_f[:, :]))
            follow(dve.tensor_tensor(later[:, :, :], first[:, 1:].unsqueeze(1).broadcast_to([P, BLOCKS, EXPERTS - 1]),
                                     block_no.unsqueeze(2).broadcast_to([P, BLOCKS, EXPERTS - 1]), ALU.is_le))
            follow(dve.tensor_reduce(block_f[:, 0, :], later[:, :, :], AX.X, ALU.add))
            follow(dve.tensor_scalar(block_f[:, 1, :], block_f[:, 0, :], float(WSLOTS), float(WSLOTS), ALU.is_ge, ALU.mult))
            follow(dve.tensor_tensor(block_f[:, 2, :], block_f[:, 0, :], block_f[:, 1, :], ALU.subtract))
            follow(dve.tensor_copy(block_i[:, 0, :], block_f[:, 0, :]))
            follow(dve.tensor_copy(block_i[:, 1, :], block_f[:, 2, :]))
            dve.engine_nop().then_inc(slots_ready, 1)

            exp3_done_, gate_step_ = Awaited(dve, exp3_done, HALVES), Awaited(dve, gate_step, 2 * HALVES)
            xs_turned_ = Awaited(dve, xs_turned, 1)

            def block_steps():
                for half in range(HALVES):
                    exp3_done_.wait_ge(half + 1)
                    dve.tensor_scalar(eg[:, half, :], eg[:, half, :], 1.0, None, ALU.add).then_inc(gate_step, 1)
                    gate_step_.wait_ge(2 * half + 1)
                    dve.reciprocal(eg[:, half, :], eg[:, half, :]).then_inc(gate_step, 1)
                    gate_step_.wait_ge(2 * half + 2)
                    dve.tensor_tensor(u[:, half, :], psum[:, 2 * half, :], eg[:, half, :], ALU.mult).then_inc(gated, 1)
                for awaited in (exp3_done_, gate_step_, xs_turned_):
                    awaited.next_turn()

            dve.wait_ge(xs_in, 16)
            dve.tensor_copy(x_now[:, :], xs[:, 0, :]).then_inc(x_picked, 1)
            for awaited in (exp3_done_, gate_step_, xs_turned_):
                awaited.enter_loop()
            with dve.Fori(0, BLOCKS - 1) as k:
                xs_turned_.wait_ge(1)
                dve.tensor_copy(x_now[:, :], xs[:, bass.ds(k + 1, 1), :].rearrange("p o c -> p (o c)")
                                ).then_inc(x_picked, 1)
                block_steps()
            block_steps()
            for i in range(TT):
                dve.wait_ge(y_back[i // 4], 64)
                dve.tensor_tensor(h2[:, i, :], h2[:, i, :], yg[:, i, :], ALU.add).then_inc(final, 1)


def vit_tower(nc, x, wave_w, wave_b, wq_t, wk_t, wv_t, qkv_b, ext_k, ext_v, wo_t, bo, router_w, router_b, w1, b1, w2,
              b2, out):
    def scratch(name, shape, dt=F32):
        return nc.dram_tensor(name, shape, dt, kind="Internal").ap()

    h_dram = scratch("h_scratch", [TOK, D])
    q_dram = scratch("q_scratch", [WINDOWS, NPART, D, BG, WQ], BF16)
    k_dram = scratch("k_scratch", [NPART, D, B, S], BF16)
    ek_dram = scratch("ek_scratch", [STACK, EXT], BF16)
    ev_dram = scratch("ev_scratch", [EXT, NPART, HD], BF16)
    rx_dram = scratch("rx_scratch", [NWIN, KC, P, WQ * NPART * HD], BF16)
    rel_dram = scratch("rel_scratch", [GROUPS, NB, 2, PAIRS * S])
    rv_dram = scratch("rv_scratch", [WINDOWS, NB, 2, PAIRS * HD])
    b1p_dram = scratch("b1_scratch", [NPART, EXPERTS * 2 * HID], BF16)
    b2p_dram = scratch("b2_scratch", [NPART, EXPERTS * D], BF16)
    xs_dram = scratch("xs_scratch", [BLOCKS * P, D])
    ys_dram = scratch("ys_scratch", [BLOCKS * P, D])
    with ExitStack() as ctx:
        ident = ctx.enter_context(nc.sbuf_tensor("ident", [P, P], F32))
        o_all = ctx.enter_context(nc.sbuf_tensor("o_all", [P, WINDOWS, TILES, HD], F32))
        sums = ctx.enter_context(nc.sbuf_tensor("sums", [P, WINDOWS, TILES], F32))
        with nc.sbuf_tensor("v_parts", [P, NPART, KC, B, D], BF16) as v_parts:
            tokens_stage(nc, x, wave_w, wave_b, wq_t, wk_t, wv_t, qkv_b, ext_k, ext_v, h_dram, v_parts, q_dram, k_dram,
                         ek_dram, ev_dram, rx_dram, ident)
            attention_stage(nc, q_dram, k_dram, ek_dram, rx_dram, rel_dram, rv_dram, v_parts, ident, o_all, sums)
        feed_forward_stage(nc, h_dram, rv_dram, o_all, sums, ident, wo_t, bo, router_w, router_b, w1, b1, w2, b2,
                           b1p_dram, b2p_dram, xs_dram, ys_dram, out)


def lay_out(given):
    rows = S // ROWS
    wave = [given["L0_tok_Wa"].reshape(rows, -1)]
    for level in (1, 2, 3):
        w = given[f"L0_tok_Wd{level}"]
        wave.append(w.reshape(3, rows, -1, 3).transpose(1, 3, 0, 2).reshape(rows, -1))
    shift = np.arange(EXT)
    reach = (given["L0_attn_rel_k"].shape[0] - 1) // 2
    rows = np.clip(shift - (S - 1), -reach, reach) + reach
    laid = {
        "x": given["x"],
        "wave_w": np.concatenate(wave, axis=1),
        "wave_b": np.concatenate([given[f"L0_tok_{n}"] for n in ("ba", "bd1", "bd2", "bd3")]),
        "wq_t": given["L0_attn_Wq"].T,
        "wk_t": given["L0_attn_Wk"].T,
        "wv_t": given["L0_attn_Wv"].T,
        "qkv_b": np.stack([given["L0_attn_bq"], given["L0_attn_bk"], given["L0_attn_bv"]]),
        "ext_k": given["L0_attn_rel_k"][rows].T,
        "ext_v": given["L0_attn_rel_v"][rows],
        "wo_t": given["L0_attn_Wo"].T,
        "bo": given["L0_attn_bo"],
    }
    for n in ("router_w", "router_b", "w1", "b1", "w2", "b2"):
        laid[n] = given[f"L0_ffn_{n}"]
    return {n: np.ascontiguousarray(a) for n, a in laid.items()}


def kernel(**inputs):
    import concourse.bacc as bacc
    from concourse.bass_utils import run_bass_kernel_spmd

    arrays = lay_out({n: np.asarray(a) for n, a in inputs.items()})
    nc = bacc.Bacc("TRN2", target_bir_lowering=False, num_devices=1)
    args = [nc.dram_tensor("in_" + n, a.shape, mybir.dt.from_np(a.dtype), kind="ExternalInput").ap()
            for n, a in arrays.items()]
    args.append(nc.dram_tensor("out", [TOK, D], F32, kind="ExternalOutput").ap())
    vit_tower(nc, *args)
    result = run_bass_kernel_spmd(nc, [{"in_" + n: a for n, a in arrays.items()}], core_ids=[0])
    return result.results[0]["out"].reshape(B, S, D)
```

```python
import numpy as np
from contextlib import ExitStack

import concourse.bass as bass
from concourse import mybir

F32 = mybir.dt.float32
F32R = mybir.dt.float32r
BF16 = mybir.dt.bfloat16
F16 = mybir.dt.float16
I32 = mybir.dt.int32
U32 = mybir.dt.uint32
ALU = mybir.AluOpType
ACT = mybir.ActivationFunctionType
AX = mybir.AxisListType

P = 128
B, S, D = 8, 256, 256
TOK = B * S
TT = TOK // P
KC = D // P
HEADS, HD = 16, 16
EXPERTS, HID = 8, 1024
EPS = 1e-5
LEVELS = 3
ROWS = 8
HALF = 2
NPART = 3
Q_TERMS = (0, 0, 1, 1, 0, 2)
K_TERMS = (0, 1, 0, 1, 2, 0)
STACK = len(Q_TERMS) * HD
EXT = 512
WQ = 64
NWIN = S // WQ
BG = 4
GROUPS = B // BG
WINDOWS = GROUPS * NWIN


def wavelet_columns():
    at, found = 1, {0: (0, ROWS * D >> (2 * LEVELS))}
    at = found[0][1]
    for level in range(LEVELS, 0, -1):
        n = 3 * (ROWS * D >> (2 * level))
        found[level] = (at, n)
        at += 3 * n
    return found, at


def tokens_stage(nc, x, wave_w, wave_b, wq_t, wk_t, wv_t, qkv_b, ext_k, ext_v, h_dram, v_parts, q_dram, k_dram,
                 ek_dram, ev_dram, ident):
    columns, wave_n = wavelet_columns()
    with ExitStack() as ctx:
        def sb(name, shape, dt=F32):
            return ctx.enter_context(nc.sbuf_tensor(name, shape, dt))

        def sem(name):
            return ctx.enter_context(nc.semaphore(name))

        img = sb("img", [P, HALF, ROWS * D])
        wave = sb("wave", [P, wave_n])
        wbias = sb("wbias", [P, 10])
        blocks = sb("blocks", [P, 4, 32])
        band = {n: sb(f"band{n}", [P, HALF, 4, ROWS * D >> (2 * n)]) for n in (1, 2, 3)}
        mix = sb("mix", [P, HALF, 2, ROWS * D // 2])
        junk = sb("junk", [P, 3 * ROWS * D // 4])
        dots = sb("dots", [P, HALF, 10])
        z = sb("z", [P, HALF, 10])
        zmax = sb("zmax", [P, HALF, 3])
        e = sb("e", [P, HALF, 10])
        esum = sb("esum", [P, HALF, 4])
        einv = sb("einv", [P, HALF, 4])
        gate = sb("gate", [P, HALF, 10])
        stats = sb("stats", [P, TT, 6])
        mv = sb("mv", [P, TT, 2])
        var = sb("var", [P, TT])
        sd = sb("sd", [P, TT])
        rs = sb("rs", [P, 4, TT])
        xnt = sb("xnt", [P, KC, TOK])
        wqk = sb("wqk", [P, 2, KC, D])
        wv = sb("wv", [P, KC, D])
        qk_b = sb("qk_b", [P, 2, KC])
        v_b = sb("v_b", [P, D])
        full = sb("full", [P, 2, 512])
        rest = sb("rest", [P, 2, 512])
        parts = sb("parts", [P, 2, NPART, 512], BF16)
        vfull = sb("vfull", [P, 2, KC, D])
        vrest = sb("vrest", [P, 2, KC, D])
        ek = sb("ek", [HD, EXT])
        ek3 = sb("ek3", [HD, NPART, EXT], BF16)
        ev = sb("ev", [P, EXT * HD // P])
        ev3 = sb("ev3", [P, EXT // P, NPART, HD], BF16)
        h_sb = sb("h_sb", [P, HALF, ROWS, D])
        ps_dots = ctx.enter_context(nc.psum_tensor("ps_dots", [P, 512], F32))
        ps_t = ctx.enter_context(nc.psum_tensor("ps_t", [P, 2, 512], F32))
        ps_p = ctx.enter_context(nc.psum_tensor("ps_p", [P, 2, 512], F32))
        ps_v = ctx.enter_context(nc.psum_tensor("ps_v", [P, 2, 512], F32))

        x_in = [sem(f"x_in{t}") for t in range(HALF)]
        wave_in = sem("wave_in")
        w_in = sem("w_in")
        ext_in = sem("ext_in")
        const_done = sem("const_done")
        haar = sem("haar")
        dots_done = sem("dots_done")
        dots_summed = sem("dots_summed")
        exp_ready = sem("exp_ready")
        exp_done = sem("exp_done")
        gate_ready = sem("gate_ready")
        scaled = sem("scaled")
        var_ready = sem("var_ready")
        sd_done = sem("sd_done")
        norm_done = sem("norm_done")
        turned = sem("turned")
        turned_out = sem("turned_out")
        proj_done = sem("proj_done")
        full_done = sem("full_done")
        split_done = sem("split_done")
        parts_sent = [sem(f"parts_sent{i}") for i in range(2)]
        vproj_done = sem("vproj_done")
        vhigh_done = sem("vhigh_done")
        v_step = sem("v_step")
        h_sent = sem("h_sent")
        ext_split = sem("ext_split")
        ext_step = sem("ext_step")
        ext_sent = sem("ext_sent")

        block = ctx.enter_context(nc.Block())
        rows_v = x.rearrange("b (r j) c o -> (b r) (j c o)", j=ROWS)
        NS = TOK // 512
        slices = [(m, c, s) for s in range(NS) for m in range(2) for c in range(KC)]

        @block.sync
        def _(sp):
            for t in range(HALF):
                sp.dma_start(img[:, t, :], rows_v[t * P:(t + 1) * P, :]).then_inc(x_in[t], 16)
            for i in range(4):
                sp.dma_start(wave[32 * i:32 * i + 32, :], wave_w).then_inc(wave_in, 16)
            sp.dma_start(wbias[:, :], wave_b.rearrange("(a n) -> a n", a=1).broadcast_to([P, 10])).then_inc(wave_in, 16)
            sp.dma_start(ek[:, :], ext_k).then_inc(ext_in, 16)
            sp.dma_start(ev[:, :], ext_v.rearrange("(p n) d -> p (n d)", p=P)).then_inc(ext_in, 16)
            for m, w in enumerate((wq_t, wk_t)):
                sp.dma_start(wqk[:, m, :, :], w.rearrange("(k p) n -> p k n", p=P)).then_inc(w_in, 16)
            sp.dma_start(wv[:, :, :], wv_t.rearrange("(k p) n -> p k n", p=P)).then_inc(w_in, 16)
            for m in range(2):
                sp.dma_start(qk_b[:, m, :], qkv_b[m].rearrange("(k p) -> p k", p=P),
                             allow_slow_non_contiguous=True).then_inc(w_in, 16)
            sp.dma_start(v_b[:, :], qkv_b[2:3, :].broadcast_to([P, D])).then_inc(w_in, 16)
            sp.wait_ge(norm_done, 1)
            sp.dma_start(h_dram.rearrange("(t p j) c -> p t j c", t=HALF, j=ROWS), h_sb[:, :, :, :]).then_inc(h_sent, 16)
            sp.wait_ge(ext_split, 2)
            for t in range(len(K_TERMS)):
                sp.dma_start(ek_dram[t * HD:(t + 1) * HD, :], ek3[:, K_TERMS[t], :]).then_inc(ext_sent, 16)
            sp.dma_start(ev_dram.rearrange("(p n) a d -> p n a d", p=P), ev3[:, :, :, :]).then_inc(ext_sent, 16)
            sent = [0, 0]
            for i, (m, c, s) in enumerate(slices):
                sp.wait_ge(split_done, i + 1)
                rows = slice(c * P, (c + 1) * P)
                for n in range(NPART):
                    if m:
                        sp.dma_start(k_dram[n, rows, 2 * s:2 * s + 2, :].rearrange("r b k -> r (b k)"),
                                     parts[:, i % 2, n, :]).then_inc(parts_sent[i % 2], 16)
                        sent[i % 2] += 1
                        continue
                    for b in (2 * s, 2 * s + 1):
                        first = NWIN * (b // BG)
                        sp.dma_start(q_dram[first:first + NWIN, n, rows, b % BG, :].rearrange("w r q -> r w q"),
                                     parts[:, i % 2, n, (b % 2) * S:(b % 2 + 1) * S].rearrange(
                                         "p (w q) -> p w q", q=WQ)).then_inc(parts_sent[i % 2], 16)
                        sent[i % 2] += 1
            sp.wait_ge(h_sent, 16)
            for i in range(2):
                sp.wait_ge(parts_sent[i], 16 * sent[i])
            sp.wait_ge(ext_sent, 16 * (len(K_TERMS) + 1))

        @block.gpsimd
        def _(pool):
            pool.memset(ident[:, :], 0.0).then_inc(const_done, 1)
            pool.memset(blocks[:, :, :], 1.0).then_inc(const_done, 1)
            pool.wait_ge(const_done, 2)
            pool.affine_select(out=ident[:, :], in_=ident[:, :], compare_op=ALU.not_equal, fill=1.0, base=0,
                               pattern=[[-1, P]], channel_multiplier=1).then_inc(const_done, 1)
            pool.affine_select(out=blocks[:, :, :], in_=blocks[:, :, :], compare_op=ALU.is_ge, fill=0.0, base=0,
                               pattern=[[-32, 4], [0, 32]], channel_multiplier=1).then_inc(const_done, 1)
            pool.wait_ge(const_done, 4)
            pool.affine_select(out=blocks[:, :, :], in_=blocks[:, :, :], compare_op=ALU.is_ge, fill=0.0, base=31,
                               pattern=[[32, 4], [0, 32]], channel_multiplier=-1).then_inc(const_done, 1)

        @block.vector
        def _(dve):
            n_haar = [0]

            def stepped(ins):
                n_haar[0] += 1
                ins.then_inc(haar, 1)
                return n_haar[0]

            def source(level, t):
                return img[:, t, :] if level == 1 else band[level - 1][:, t, 0, :]

            for t in range(HALF):
                dve.wait_ge(x_in[t], 16)
                for level in (1, 2, 3):
                    n = ROWS * D >> (2 * level - 2)
                    cols = D >> level
                    pair = source(level, t).rearrange("p (n two) -> p n two", two=2)
                    m = mix[:, t, :, 0:n // 2]
                    stepped(dve.tensor_tensor(m[:, 0, :], pair[:, :, 0], pair[:, :, 1], ALU.add))
                    dve.wait_ge(haar, stepped(dve.tensor_tensor(m[:, 1, :], pair[:, :, 0], pair[:, :, 1], ALU.subtract)))
                    m4 = m.rearrange("p a (r two c) -> p a r two c", two=2, c=cols)
                    out = band[level][:, t, :, :].rearrange("p a (r c) -> p a r c", c=cols)
                    stepped(dve.tensor_tensor(out[:, 0:4:2], m4[:, :, :, 0, :], m4[:, :, :, 1, :], ALU.add))
                    dve.wait_ge(haar, stepped(dve.tensor_tensor(out[:, 1:4:2], m4[:, :, :, 0, :], m4[:, :, :, 1, :],
                                                                ALU.subtract)))
                at, n = columns[0]
                if t == 0:
                    dve.wait_ge(wave_in, 16 * 5)
                dve.wait_ge(haar, stepped(dve.tensor_tensor_reduce(
                    junk[:, 0:n], band[3][:, t, 0, :], wave[:, at:at + n], 0.5 ** LEVELS, 0.0, ALU.mult, ALU.add,
                    dots[:, t, 0:1])))
                for level in (3, 2, 1):
                    at, n = columns[level]
                    for c in range(3):
                        col = 1 + 3 * (3 - level) + c
                        dve.wait_ge(haar, stepped(dve.tensor_tensor_reduce(
                            junk[:, 0:n], band[level][:, t, 1:4, :].rearrange("p a n -> p (a n)"),
                            wave[:, at + c * n:at + (c + 1) * n], 0.5 ** level, 0.0, ALU.mult, ALU.add,
                            dots[:, t, col:col + 1])))
            dve.engine_nop().then_inc(dots_done, 1)
            dve.wait_ge(dots_summed, 1)
            s1 = stepped(dve.tensor_tensor(z[:, :, :], ps_dots[:, 0:20].rearrange("p (t n) -> p t n", t=HALF),
                                           wbias[:, :].unsqueeze(1).broadcast_to([P, HALF, 10]), ALU.add))
            dve.wait_ge(haar, s1)
            z3 = z[:, :, 1:10].rearrange("p t (l c) -> p t l c", c=3)
            e3 = e[:, :, 1:10].rearrange("p t (l c) -> p t l c", c=3)
            dve.wait_ge(haar, stepped(dve.tensor_reduce(zmax[:, :, :], z3, AX.X, ALU.max)))
            for t in range(HALF):
                stepped(dve.tensor_tensor(z3[:, t], z3[:, t], zmax[:, t, :].unsqueeze(2).broadcast_to([P, 3, 3]), ALU.subtract))
            dve.wait_ge(haar, stepped(dve.tensor_scalar(z[:, :, 0:1], z[:, :, 0:1], -1.0, None, ALU.mult)))
            dve.engine_nop().then_inc(exp_ready, 1)
            dve.wait_ge(exp_done, 1)
            stepped(dve.tensor_reduce(esum[:, :, 1:4], e3, AX.X, ALU.add))
            dve.wait_ge(haar, stepped(dve.tensor_scalar(esum[:, :, 0:1], e[:, :, 0:1], 1.0, None, ALU.add)))
            dve.wait_ge(haar, stepped(dve.reciprocal(einv[:, :, :], esum[:, :, :])))
            stepped(dve.tensor_scalar(gate[:, :, 0:1], einv[:, :, 0:1], 0.25 ** 3, None, ALU.mult))
            for t in range(HALF):
                for level in (3, 2, 1):
                    a = 1 + 3 * (3 - level)
                    k = stepped(dve.tensor_scalar(gate[:, t, a:a + 3], e[:, t, a:a + 3], einv[:, t, 4 - level:5 - level],
                                                  0.25 ** level, ALU.mult, ALU.mult))
            dve.wait_ge(haar, k)
            dve.engine_nop().then_inc(gate_ready, 1)
            for t in range(HALF):
                for level in (3, 2, 1):
                    dve.wait_ge(scaled, 10 * t + {3: 4, 2: 7, 1: 10}[level])
                    n = ROWS * D >> (2 * level - 2)
                    cols = D >> level
                    m = mix[:, t, :, 0:n // 2]
                    m4 = m.rearrange("p a (r two c) -> p a r two c", two=2, c=cols)
                    bd = band[level][:, t, :, :].rearrange("p a (r c) -> p a r c", c=cols)
                    stepped(dve.tensor_tensor(m4[:, :, :, 0, :], bd[:, 0:4:2], bd[:, 1:4:2], ALU.add))
                    dve.wait_ge(haar, stepped(dve.tensor_tensor(m4[:, :, :, 1, :], bd[:, 0:4:2], bd[:, 1:4:2],
                                                                ALU.subtract)))
                    out = h_sb[:, t, :, :].rearrange("p j c -> p (j c)") if level == 1 else band[level - 1][:, t, 0, :]
                    out = out.rearrange("p (n two) -> p n two", two=2)
                    stepped(dve.tensor_tensor(out[:, :, 0], m[:, 0, :], m[:, 1, :], ALU.add))
                    dve.wait_ge(haar, stepped(dve.tensor_tensor(out[:, :, 1], m[:, 0, :], m[:, 1, :], ALU.subtract)))
            for i in range(TT):
                k = stepped(dve.bn_stats(stats[:, i, :], h_sb[:, i // ROWS, i % ROWS, :]))
            dve.wait_ge(haar, k)
            for i in range(TT):
                k = stepped(dve.bn_aggr(mv[:, i, :], stats[:, i, :]))
            dve.wait_ge(haar, k)
            dve.wait_ge(haar, stepped(dve.tensor_scalar(var[:, :], mv[:, :, 1], EPS, None, ALU.add)))
            dve.engine_nop().then_inc(var_ready, 1)
            dve.wait_ge(sd_done, 1)
            dve.wait_ge(haar, stepped(dve.reciprocal(rs[:, 0, :], sd[:, :])))
            dve.wait_ge(haar, stepped(dve.tensor_tensor(rs[:, 1, :], rs[:, 0, :], rs[:, 0, :], ALU.mult)))
            dve.wait_ge(haar, stepped(dve.tensor_tensor(rs[:, 2, :], rs[:, 1, :], var[:, :], ALU.mult)))
            dve.wait_ge(haar, stepped(dve.tensor_scalar(rs[:, 1, :], rs[:, 2, :], -0.5, 1.5, ALU.mult, ALU.add)))
            dve.wait_ge(haar, stepped(dve.tensor_tensor(rs[:, 3, :], rs[:, 0, :], rs[:, 1, :], ALU.mult)))
            for i in range(TT):
                t, j = i // ROWS, i % ROWS
                dve.tensor_scalar(img[:, t, j * D:(j + 1) * D], h_sb[:, t, j, :], mv[:, i, 0:1], rs[:, 3, i:i + 1],
                                  ALU.subtract, ALU.mult).then_inc(norm_done, 1)
            dve.wait_ge(ext_in, 32)
            n_ext = 0
            ev_v = ev[:, :].rearrange("p (n d) -> p n d", d=HD)
            for full_ap, part_aps in ((ek[:, :], [ek3[:, n, :] for n in range(NPART)]),
                                      (ev_v, [ev3[:, :, n, :] for n in range(NPART)])):
                for n in range(NPART):
                    dve.tensor_copy(part_aps[n], full_ap).then_inc(ext_step, 1)
                    n_ext += 1
                    dve.wait_ge(ext_step, n_ext)
                    if n < NPART - 1:
                        dve.tensor_tensor(full_ap, full_ap, part_aps[n], ALU.subtract).then_inc(ext_step, 1)
                        n_ext += 1
                        dve.wait_ge(ext_step, n_ext)
                dve.engine_nop().then_inc(ext_split, 1)
            sent = [0, 0]
            for i, (m, c, s) in enumerate(slices):
                dve.wait_ge(full_done, 2 * (i + 1))
                if i >= 2:
                    dve.wait_ge(parts_sent[i % 2], 16 * sent[i % 2])
                sent[i % 2] += NPART * (1 if m else 2)
                dve.wait_ge(haar, stepped(dve.tensor_tensor(rest[:, i % 2, :], full[:, i % 2, :], parts[:, i % 2, 0, :],
                                                            ALU.subtract)))
                dve.wait_ge(haar, stepped(dve.tensor_copy(parts[:, i % 2, 1, :], rest[:, i % 2, :])))
                dve.tensor_tensor(parts[:, i % 2, 2, :], rest[:, i % 2, :], parts[:, i % 2, 1, :],
                                  ALU.subtract).then_inc(split_done, 1)
            for b in range(B):
                two = v_b[:, :].unsqueeze(1).broadcast_to([P, KC, D])
                full_b, rest_b = vfull[:, b % 2, :, :], vrest[:, b % 2, :, :]
                dve.wait_ge(vproj_done, KC * (b + 1))
                dve.tensor_tensor(full_b, ps_v[:, b % 2, :].rearrange("p (c n) -> p c n", c=KC), two,
                                  ALU.add).then_inc(v_step, 1)
                dve.wait_ge(v_step, 5 * b + 1)
                dve.tensor_copy(v_parts[:, 0, :, b, :], full_b).then_inc(v_step, 1)
                dve.wait_ge(v_step, 5 * b + 2)
                dve.tensor_tensor(rest_b, full_b, v_parts[:, 0, :, b, :], ALU.subtract).then_inc(v_step, 1)
                dve.wait_ge(v_step, 5 * b + 3)
                dve.tensor_copy(v_parts[:, 1, :, b, :], rest_b).then_inc(v_step, 1)
                dve.wait_ge(v_step, 5 * b + 4)
                dve.tensor_tensor(v_parts[:, 2, :, b, :], rest_b, v_parts[:, 1, :, b, :],
                                  ALU.subtract).then_inc(v_step, 1)

        @block.scalar
        def _(act):
            act.wait_ge(exp_ready, 1)
            act.activation(e[:, :, :], z[:, :, :], ACT.Exp).then_inc(exp_done, 1)
            act.wait_ge(gate_ready, 1)
            for t in range(HALF):
                act.activation(band[3][:, t, 0, :], band[3][:, t, 0, :], ACT.Copy, scale=gate[:, t, 0:1]).then_inc(scaled, 1)
                for level in (3, 2, 1):
                    for c in range(3):
                        col = 1 + 3 * (3 - level) + c
                        act.activation(band[level][:, t, 1 + c, :], band[level][:, t, 1 + c, :], ACT.Copy,
                                       scale=gate[:, t, col:col + 1]).then_inc(scaled, 1)
            act.wait_ge(var_ready, 1)
            act.activation(sd[:, :], var[:, :], ACT.Sqrt).then_inc(sd_done, 1)
            xnt_v = xnt[:, :, :].rearrange("f k (t p j) -> f k t p j", t=HALF, j=ROWS)
            for i in range(TT // 2):
                t, j = 2 * i // ROWS, 2 * i % ROWS
                act.wait_ge(turned, i + 1)
                for jj in range(2):
                    ins = act.activation(xnt_v[:, :, t, :, j + jj],
                                   ps_t[:, i % 2, jj * D:(jj + 1) * D].rearrange("f (k p) -> f k p", k=KC),
                                   ACT.Copy)
                ins.then_inc(turned_out, 1)
            act.wait_ge(w_in, 16 * 6)
            for i, (m, c, s) in enumerate(slices):
                act.wait_ge(proj_done, i + 1)
                if i >= 2:
                    act.wait_ge(split_done, i - 1)
                act.activation(full[:, i % 2, :], ps_p[:, i % 2, :], ACT.Identity, bias=qk_b[:, m, c:c + 1]).then_inc(full_done, 1)
                if i >= 2:
                    need = NPART * sum(1 if slices[k][0] else 2 for k in range(i % 2, i, 2))
                    act.wait_ge(parts_sent[i % 2], 16 * need)
                act.activation(parts[:, i % 2, 0, :], ps_p[:, i % 2, :], ACT.Identity, bias=qk_b[:, m, c:c + 1]).then_inc(full_done, 1)

        @block.tensor
        def _(pe):
            pe.wait_ge(const_done, 5)
            pe.wait_ge(dots_done, 1)
            pe.matmul(ps_dots[:, 0:20], blocks[:, :, :].rearrange("p a b -> p (a b)"),
                      dots[:, :, :].rearrange("p t n -> p (t n)"), start=True, stop=True).then_inc(dots_summed, 1)
            for i in range(TT // 2):
                if i >= 2:
                    pe.wait_ge(turned_out, i - 1)
                for jj in range(2):
                    n = 2 * i + jj
                    pe.wait_ge(norm_done, n + 1)
                    for k in range(KC):
                        at = (n % ROWS) * D + k * P
                        ins = pe.transpose(ps_t[:, i % 2, jj * D + k * P:jj * D + (k + 1) * P],
                                           img[:, n // ROWS, at:at + P], ident[:, :])
                ins.then_inc(turned, 1)
            pe.wait_ge(turned_out, TT // 2)
            pe.wait_ge(w_in, 16 * 6)
            for i, (m, c, s) in enumerate(slices):
                if i >= 2:
                    pe.wait_ge(full_done, 2 * (i - 1))
                for k in range(KC):
                    ins = pe.matmul(ps_p[:, i % 2, :], wqk[:, m, k, c * P:(c + 1) * P], xnt[:, k, s * 512:(s + 1) * 512],
                                    start=(k == 0), stop=(k == KC - 1))
                ins.then_inc(proj_done, 1)
            for i in range(TT):
                b, c = i // KC, i % KC
                if b >= 2 and c == 0:
                    pe.wait_ge(v_step, 5 * (b - 2) + 1)
                for k in range(KC):
                    ins = pe.matmul(ps_v[:, b % 2, c * D:(c + 1) * D], xnt[:, k, i * P:(i + 1) * P], wv[:, k, :],
                                    start=(k == 0), stop=(k == KC - 1))
                ins.then_inc(vproj_done, 1)


NB = BG * HEADS
TILES = NB // 2
AHEAD = 4
RSLOTS = 4
SLOTS = 2
PAIRS = WQ // 2
EXTW = WQ - 1 + S + 1
SCALE = float(HD) ** -0.5
RING = 4
TURN_LAG, HI_LAG, LO_LAG, PV_LAG = 3, 3, 5, 9
QUAD = 4
CHUNKS = 4


ONE = 1


class Awaited:

    def __init__(self, eng, sem, a_turn, start=0):
        self.eng, self.sem, self.a_turn, self.start, self.base = eng, sem, a_turn, start, None

    def enter_loop(self):
        self.base = self.eng.alloc_register(f"{self.sem.name}_base_{self.eng.engine.name}")
        self.value = self.eng.alloc_register(f"{self.sem.name}_value_{self.eng.engine.name}")
        self.eng.reg_mov(self.base, self.start)

    def wait_ge(self, more):
        if self.base is None:
            self.eng.wait_ge(self.sem, self.start + more)
        elif more == 0:
            self.eng.wait_ge(self.sem, self.base)
        else:
            self.eng.reg_add(self.value, self.base, more)
            self.eng.wait_ge(self.sem, self.value)

    def next_turn(self):
        if self.base is None:
            self.start += self.a_turn
        else:
            self.eng.reg_add(self.base, self.base, self.a_turn)


def attention_stage(nc, q_dram, k_dram, ek_dram, ev_dram, rel_dram, rv_dram, v_parts, ident, o_all, sums):
    with ExitStack() as ctx:
        def sb(name, shape, dt=F32):
            return ctx.enter_context(nc.sbuf_tensor(name, shape, dt))

        def sem(name):
            return ctx.enter_context(nc.semaphore(name))

        k_st = sb("k_st", [STACK, GROUPS, HEADS, BG, S], BF16)
        q_st = [sb(f"q_st{i}", [STACK, HEADS, BG, WQ], BF16) for i in range(2)]
        e_st = [sb(f"e_st{i}", [STACK, EXTW], BF16) for i in range(2)]
        rpv = sb("rpv", [P, KC, WQ, NPART, HD], BF16)
        pt_hi = sb("pt_hi", [P, KC, NB * WQ], F16)
        pt_lo = sb("pt_lo", [P, KC, NB * WQ], F16)
        rel_out = sb("rel_out", [P, RSLOTS, 2, 2 * S])
        rel_in = sb("rel_in", [P, SLOTS, QUAD, S])
        scores = sb("scores", [P, RING, S])
        probs = sb("probs", [P, RING, S])
        low = sb("low", [P, 2, TILES])
        rv = sb("rv", [P, PAIRS, HD])
        idle_p = sb("idle_p", [1, 4])
        rv_rows = sb("rv_rows", [P, TILES, HD])
        idle = sb("idle", [1, TILES // 2 + AHEAD // 2])
        ps_rel = ctx.enter_context(nc.psum_tensor("ps_rel", [P, 2, 512], F32))
        ps_sc = ctx.enter_context(nc.psum_tensor("ps_sc", [P, 4, S], F32))
        ps_pt = ctx.enter_context(nc.psum_tensor("ps_pt", [P, 2, 2, KC, P], F32))
        ps_o = ctx.enter_context(nc.psum_tensor("ps_o", [P, 2, 512], F32))

        k_loaded = [sem(f"k_loaded{b}") for b in range(GROUPS)]
        q_loaded = [sem(f"q_loaded{i}") for i in range(2)]
        rpv_loaded = sem("rpv_loaded")
        rel_made = sem("rel_made")
        rel_copied = sem("rel_copied")
        rel_sent = [[sem(f"rel_sent{i}{j}") for j in range(RSLOTS)] for i in range(2)]
        rel_back = [sem(f"rel_back{i}") for i in range(SLOTS)]
        content_done = sem("content_done")
        added = sem("added")
        exp_done = sem("exp_done2")
        turned = sem("turned2")
        hi_done = sem("hi_done")
        lo_done = sem("lo_done")
        acc_made = sem("acc_made")
        acc_out = sem("acc_out")
        rv_sent = sem("rv_sent")
        idle_set = sem("idle_set")
        rv_back = sem("rv_back")
        rv_added = sem("rv_added")
        rv_free = sem("rv_free")
        START = SLOTS * QUAD
        QUADS = TILES // QUAD
        SENT = QUADS // RSLOTS * 32
        ACCS = QUADS + CHUNKS

        block = ctx.enter_context(nc.Block())

        def load_window(eng, w, g):
            for t in range(len(Q_TERMS)):
                eng.dma_start(q_st[g][t * HD:(t + 1) * HD, :, :, :].rearrange("d h b q -> d h (b q)"),
                              q_dram[bass.ds(w + g * NWIN, 1), Q_TERMS[t], :, :, :].rearrange(
                                  "n (h d) b q -> d (n h) (b q)", d=HD)).then_inc(q_loaded[g], 16)
            eng.dma_start(e_st[g][:, :], ek_dram[:, bass.ds((NWIN - 1 - w) * WQ, EXTW)]).then_inc(q_loaded[g], 16)

        LOADS = 16 * (len(Q_TERMS) + 1)

        @block.gpsimd
        def _(pool):
            pool.memset(idle_p[:, 0:1], 0.0).then_inc(idle_set, 1)
            for g in range(GROUPS):
                load_window(pool, 0, g)
            pool.wait_ge(idle_set, 1)
            with pool.Fori(0, NWIN) as w:
                for g in range(GROUPS):
                    n = GROUPS * w + g
                    if g == 0:
                        pool.wait_ge(acc_made, ACCS * n + ONE)
                        pool.wait_ge(q_loaded[0], LOADS)
                        pool.tensor_tensor(idle_p[:, 3:4], idle_p[:, 0:1], idle_p[:, 0:1], ALU.add).then_inc(idle_set, 1)
                        for c in range(KC):
                            row = NPART * HD
                            pool.dma_start(rpv[:, c, :, :, :].rearrange("p q a d -> p (q a d)"),
                                           bass.AP(ev_dram.tensor, ((NWIN - 1 - w) * WQ + c * P) * row,
                                                   [[row, P], [1, WQ * row]])).then_inc(rpv_loaded, 16)
                    pool.wait_ge(content_done, TILES * (n + 1))
                    pool.wait_ge(q_loaded[0], LOADS)
                    load_window(pool, (w + 1) % NWIN, g)
                    pool.wait_ge(acc_out, ACCS * (n + 1) + ONE)
                    pool.wait_ge(q_loaded[0], LOADS)
                    for half in range(2):
                        pool.dma_start(rv_dram[bass.ds(n, 1), :, half, :].rearrange("n r x -> (n r) x"),
                                       rv[half * NB:(half + 1) * NB, :, :].rearrange("r q d -> r (q d)")).then_inc(rv_sent, 16)
                    pool.wait_ge(rv_sent, 32 * (n + 1))
                    pool.wait_ge(rv_added, n + ONE)
                    pool.tensor_tensor(idle_p[:, 1:2], idle_p[:, 0:1], idle_p[:, 0:1], ALU.add).then_inc(rv_free, 1)
                    pool.dma_start(rv_rows[:, :, :],
                                   rv_dram[bass.ds(n, 1)].rearrange("n (t u) v (q d) -> (n u v q) t d", u=2, d=HD)
                                   ).then_inc(rv_back, 16)
                    pool.wait_ge(rv_back, 16 * (n + 1))
                    pool.tensor_tensor(idle_p[:, 2:3], idle_p[:, 0:1], idle_p[:, 0:1], ALU.add).then_inc(idle_set, 1)
                    pool.tensor_tensor(o_all[:, bass.ds(n, 1), :, :].rearrange("p o t d -> p (o t) d"),
                                       o_all[:, bass.ds(n, 1), :, :].rearrange("p o t d -> p (o t) d"),
                                       rv_rows[:, :, :], ALU.add).then_inc(rv_added, 1)
            for g in range(GROUPS):
                pool.wait_ge(q_loaded[g], LOADS * (NWIN + 1))

        @block.sync
        def _(sp):
            for g in range(GROUPS):
                for t in range(len(K_TERMS)):
                    sp.dma_start(k_st[t * HD:(t + 1) * HD, g, :, :, :].rearrange("d h b k -> d h (b k)"),
                                 k_dram[K_TERMS[t], :, g * BG:(g + 1) * BG, :].rearrange("(h d) b k -> d h (b k)", d=HD)
                                 ).then_inc(k_loaded[g], 16)

            def send(g, base, j):
                sp.wait_ge(rel_copied, base + 2 * (j + 1))
                for half in range(2):
                    sp.dma_start(rel_dram[g, :, half, 4 * j * S:4 * (j + 1) * S],
                                 rel_out[half * NB:(half + 1) * NB, j % RSLOTS, :, :].rearrange("r a b -> r (a b)")
                                 ).then_inc(rel_sent[g][j % RSLOTS], 16)

            for j in range(QUADS):
                send(0, 0, j)
            with sp.Fori(0, NWIN) as w:
                for g in range(GROUPS):
                    n = GROUPS * w + g
                    for slot in range(RSLOTS):
                        sp.wait_ge(rel_sent[g][slot], SENT * (w + 1))
                    rows = rel_dram[g, :, :, :].rearrange("(t u) v (q k) -> (u v q) t k", u=2, k=S)

                    def bring(j):
                        sp.wait_ge(added, TILES * n + QUAD * (j + 1))
                        sp.dma_start(rel_in[:, j % SLOTS, :, :], rows[:, QUAD * j:QUAD * (j + 1), :]
                                     ).then_inc(rel_back[j % SLOTS], 16)

                    for j in range(SLOTS):
                        bring(j)
                    for j in range(QUADS):
                        send(1 - g, TILES // 2 * (n + 1), j)
                        if j + SLOTS < QUADS:
                            bring(j + SLOTS)
            for slot in range(RSLOTS):
                sp.wait_ge(rel_sent[0][slot], SENT * (NWIN + 1))
            sp.wait_ge(added, TILES * WINDOWS + QUAD)
            sp.dma_start(rel_in[:, 0, :, :], rel_dram[0].rearrange("(t u) v (q k) -> (u v q) t k", u=2, k=S)[:, 0:QUAD, :]
                         ).then_inc(rel_back[0], 16)

        @block.tensor
        def _(pe):
            def relative(i, m):
                for half in range(2):
                    q = m + half * PAIRS
                    ins = pe.matmul(ps_rel[half * NB:(half + 1) * NB, m // 2 % 2, (m % 2) * S:(m % 2 + 1) * S],
                                    q_st[i][:, :, :, q].rearrange("s h b -> s (h b)"),
                                    e_st[i][:, WQ - 1 - q:WQ - 1 - q + S], start=True, stop=True)
                if m % 2:
                    ins.then_inc(rel_made, 1)

            pe.wait_ge(q_loaded[0], LOADS)
            for m in range(PAIRS):
                if m >= 4 and m % 2 == 0:
                    pe.wait_ge(rel_copied, m // 2 - 1)
                relative(0, m)
            pe.wait_ge(k_loaded[0], 16 * len(K_TERMS))
            for t in range(AHEAD):
                for u in range(2):
                    ins = pe.matmul(ps_sc[u * WQ:(u + 1) * WQ, t, :], q_st[0][:, t // 2, 2 * (t % 2) + u, :],
                                    k_st[:, 0, t // 2, 2 * (t % 2) + u, :], start=True, stop=True)
                ins.then_inc(content_done, 1)
            added_, exp_, lo_ = (Awaited(pe, sem, per, start) for sem, per, start in (
                (added, TILES, START), (exp_done, TILES, RING - 1), (lo_done, TILES // 2, ONE)))
            copied_, out_ = Awaited(pe, rel_copied, TILES // 2, TILES // 2), Awaited(pe, acc_out, ACCS, ONE)
            for awaited in (added_, exp_, lo_, copied_, out_):
                awaited.enter_loop()
            with pe.Fori(0, NWIN) as w:
                for g in range(GROUPS):
                    n = GROUPS * w + g

                    def content(t, g=g):
                        h, b = t % TILES // 2, 2 * (t % 2)
                        if t % 2 == 0:
                            added_.wait_ge(t - 2)
                        for u in range(2):
                            ins = pe.matmul(ps_sc[u * WQ:(u + 1) * WQ, t % 4, :], q_st[g][:, h, b + u, :],
                                            k_st[:, g, h, b + u, :], start=True, stop=True)
                        ins.then_inc(content_done, 1)

                    def turn(t):
                        exp_.wait_ge(t + 1)
                        if t % 2 == 0:
                            lo_.wait_ge(max(t // 2 - 1, 0))
                        for c in range(KC):
                            ins = pe.transpose(ps_pt[:, t // 2 % 2, t % 2, c, :], probs[:, t % RING, c * P:(c + 1) * P],
                                               ident[:, :])
                        ins.then_inc(turned, 1)

                    def values(t):
                        a = t // QUAD
                        if t % 2 == 0:
                            lo_.wait_ge(t // 2 + 1)
                        if t % QUAD == 0:
                            out_.wait_ge(max(a - 1, 0))
                        h, b = t // 2, 2 * (t % 2)
                        out = ps_o[:, a % 2, (t % QUAD) * 96:(t % QUAD) * 96 + 96].rearrange("p (a u d) -> p a u d", a=NPART, u=2)
                        for pt, parts in ((pt_hi, 3), (pt_lo, 2)):
                            for c in range(KC):
                                ins = pe.matmul(out[:, 0:parts, :, :], pt[:, c, t * P:(t + 1) * P],
                                                v_parts[:, 0:parts, c, g * BG + b:g * BG + b + 2,
                                                        h * HD:(h + 1) * HD],
                                                start=(parts == 3 and c == 0), stop=(parts == 2 and c == KC - 1))
                        if t % QUAD == QUAD - 1:
                            ins.then_inc(acc_made, 1)

                    for s in range(TILES + PV_LAG):
                        if s < TILES:
                            if s == 0:
                                pe.wait_ge(k_loaded[1 - g], 16 * len(K_TERMS))
                                pe.wait_ge(q_loaded[1 - g], LOADS * (w + 1 + g))
                            if s >= AHEAD and s % 2 == 0:
                                content(s)
                                content(s + 1)
                            if s % 2 == 0:
                                copied_.wait_ge(s // 2 - 1)
                            relative(1 - g, s)
                        if 0 <= s - TURN_LAG < TILES:
                            turn(s - TURN_LAG)
                        if 0 <= s - PV_LAG < TILES:
                            values(s - PV_LAG)
                    for t in range(TILES, TILES + AHEAD):
                        content(t, 1 - g)
                    pe.wait_ge(rpv_loaded, 16 * KC * (w + 1))
                    for m in range(PAIRS):
                        a = TILES // QUAD + m // 8
                        if m % 8 == 0:
                            out_.wait_ge(a - 1)
                        for pt, parts in ((pt_hi, 3), (pt_lo, 2)):
                            for c in range(KC):
                                for half in range(2):
                                    q = m + half * PAIRS
                                    cols = (m % 8) * 48
                                    ins = pe.matmul(
                                        ps_o[half * NB:(half + 1) * NB, a % 2, cols:cols + parts * HD],
                                        pt[:, c, q:NB * WQ:WQ], rpv[:, c, WQ - 1 - q, 0:parts, :].rearrange("p a d -> p (a d)"),
                                        start=(parts == 3 and c == 0), stop=(parts == 2 and c == KC - 1))
                        if m % 8 == 7:
                            ins.then_inc(acc_made, 1)
                    for awaited in (added_, exp_, lo_, copied_, out_):
                        awaited.next_turn()

        @block.scalar
        def _(act):
            def relative_out(j):
                act.activation(rel_out[:, j // 2 % RSLOTS, j % 2, :], ps_rel[:, j % 2, :], ACT.Copy).then_inc(rel_copied, 1)

            for j in range(PAIRS // 2):
                if j >= 2 * RSLOTS and j % 2 == 0:
                    act.wait_ge(rel_sent[0][j // 2 % RSLOTS], 32 * (j // 2 // RSLOTS))
                act.wait_ge(rel_made, j + 1)
                relative_out(j)
            def exponents(t, g, n):
                act.activation(probs[:, t % RING, :], scores[:, t % RING, :], ACT.Exp, scale=-1.0,
                               bias=low[:, g, t % TILES:t % TILES + 1],
                               accum_out=sums[:, bass.ds(n, 1), t % TILES:t % TILES + 1].rearrange("p o t -> p (o t)")
                               ).then_inc(exp_done, 1)

            for t in range(AHEAD):
                act.wait_ge(added, START + t + 1)
                exponents(t, 0, 0)
            added_, turned_ = Awaited(act, added, TILES, START), Awaited(act, turned, TILES, ONE)
            made_ = Awaited(act, rel_made, TILES // 2, TILES // 2)
            for awaited in (added_, turned_, made_):
                awaited.enter_loop()
            with act.Fori(0, NWIN) as w:
                for g in range(GROUPS):
                    n = GROUPS * w + g
                    for s in range(TILES + HI_LAG + 1):
                        t = s - HI_LAG
                        if 0 <= t < TILES and t % 2:
                            turned_.wait_ge(t + 1)
                            if t == 1:
                                act.wait_ge(acc_made, ACCS * n + ONE)
                            act.activation(pt_hi[:, :, (t - 1) * P:(t + 1) * P].rearrange("p c (t x) -> p t c x", t=2),
                                           ps_pt[:, t // 2 % 2, :, :, :], ACT.Copy).then_inc(hi_done, 1)
                        if s < TILES:
                            if s >= AHEAD:
                                added_.wait_ge(s + 1)
                                turned_.wait_ge(s - RING + 1)
                                exponents(s, g, n)
                            if s % 2:
                                j = s // 2
                                if j % 2 == 0:
                                    if j >= 2 * RSLOTS:
                                        act.wait_ge(rel_sent[1 - g][j // 2 % RSLOTS],
                                                    SENT * (w + g) + 32 * (j // 2 // RSLOTS))
                                    else:
                                        act.wait_ge(rel_sent[g][j // 2 % RSLOTS], SENT * (w + 1))
                                made_.wait_ge(j + 1)
                                relative_out(j)
                    for t in range(TILES, TILES + AHEAD):
                        added_.wait_ge(t + 1)
                        turned_.wait_ge(t - RING + 1)
                        exponents(t, 1 - g, n + 1)
                    for awaited in (added_, turned_, made_):
                        awaited.next_turn()

        @block.vector
        def _(dve):
            dve.engine_nop().then_inc(added, START)
            dve.engine_nop().then_inc(exp_done, RING - 1)
            for counts in (lo_done, acc_out, turned, acc_made, rv_free, rv_added):
                dve.engine_nop().then_inc(counts, ONE)
            def add(t, g):
                dve.tensor_tensor_reduce(scores[:, t % RING, :], ps_sc[:, t % 4, :],
                                         rel_in[:, t // QUAD % SLOTS, t % QUAD, :], -SCALE, 3.0e38,
                                         ALU.add, ALU.min, low[:, g, t % TILES:t % TILES + 1]).then_inc(added, 1)

            dve.wait_ge(rel_back[0], 16)
            dve.wait_ge(content_done, AHEAD)
            for t in range(AHEAD):
                add(t, 0)
            content_, exp_ = Awaited(dve, content_done, TILES), Awaited(dve, exp_done, TILES, RING - 1)
            hi_, made_ = Awaited(dve, hi_done, TILES // 2), Awaited(dve, acc_made, ACCS, ONE)
            for awaited in (content_, exp_, hi_, made_):
                awaited.enter_loop()
            with dve.Fori(0, NWIN) as w:
                for g in range(GROUPS):
                    n = GROUPS * w + g
                    def tile(t):
                        if t % QUAD == 0:
                            j = t // QUAD
                            dve.wait_ge(rel_back[j % SLOTS], 16 * (TILES // QUAD // SLOTS * n + j // SLOTS + 1))
                        if t % 2 == 0:
                            content_.wait_ge(t + 2)
                            exp_.wait_ge(t - RING + 2)
                            dve.memset(idle[:, t // 2:t // 2 + 1], 0.0)
                        add(t, g if t < TILES else 1 - g)

                    def low_halves(s):
                        t = s - LO_LAG
                        if 0 <= t < TILES and t % 2:
                            hi_.wait_ge(t // 2 + 1)
                            cols = slice((t - 1) * P, (t + 1) * P)
                            dve.tensor_tensor(pt_lo[:, :, cols].rearrange("p c (t x) -> p t c x", t=2),
                                              ps_pt[:, t // 2 % 2, :, :, :],
                                              pt_hi[:, :, cols].rearrange("p c (t x) -> p t c x", t=2),
                                              ALU.subtract).then_inc(lo_done, 1)

                    for s in range(TILES + PV_LAG + 2):
                        if LO_LAG % 2: low_halves(s)
                        if AHEAD <= s < TILES:
                            tile(s)
                        if LO_LAG % 2 == 0: low_halves(s)
                        t = s - PV_LAG - 1
                        if 0 <= t < TILES and t % QUAD == QUAD - 1:
                            a = t // QUAD
                            made_.wait_ge(a + 1)
                            acc = ps_o[:, a % 2, 0:QUAD * 96].rearrange("p (t a d) -> p t d a", t=QUAD, a=NPART)
                            for u in range(2):
                                rows = slice(u * WQ, (u + 1) * WQ)
                                ins = dve.tensor_reduce(
                                    o_all[rows, bass.ds(n, 1), QUAD * a:QUAD * (a + 1), :].rearrange("p o t d -> p (o t) d"),
                                    acc[rows, :, u * HD:(u + 1) * HD, :], AX.X, ALU.add)
                            ins.then_inc(acc_out, 1)
                    for c in range(CHUNKS):
                        a = TILES // QUAD + c
                        made_.wait_ge(a + 1)
                        if c == 0:
                            dve.wait_ge(rv_free, n + ONE)
                        dve.tensor_reduce(rv[:, 8 * c:8 * c + 8, :],
                                          ps_o[:, a % 2, 0:8 * 48].rearrange("p (q a d) -> p q d a", q=8, a=NPART),
                                          AX.X, ALU.add).then_inc(acc_out, 1)
                        if c == 0:
                            for t in range(TILES, TILES + AHEAD):
                                tile(t)
                    for awaited in (content_, exp_, hi_, made_):
                        awaited.next_turn()


BLOCKS = TOK // P + EXPERTS - 1
WSLOTS = 4
LN_GROUP = 4
HALVES = 2
HH = HID // HALVES
HC = HH // P
B1 = EXPERTS * 2 * HID // P
B2 = EXPERTS * D // P


def feed_forward_stage(nc, h_dram, o_all, sums, ident, wo_t, bo, router_w, router_b, w1, b1, w2, b2,
                       b1p_dram, b2p_dram, xs_dram, ys_dram, out):
    with ExitStack() as ctx:
        def sb(name, shape, dt=F32):
            return ctx.enter_context(nc.sbuf_tensor(name, shape, dt))

        def sem(name):
            return ctx.enter_context(nc.semaphore(name))

        h2 = sb("h2", [P, TT, D])
        xs = sb("xs", [P, BLOCKS, D])
        xn2 = xs[:, 0:TT, :]
        eg = sb("eg", [P, HALVES, HH])
        u = sb("u", [P, HALVES, HH])
        ut = sb("ut", [P, HALVES, HC, P])
        xst = sb("xst", [P, KC, P])
        zeros = sb("zeros", [P, D])
        rec = sb("rec", [P, WINDOWS, TILES])
        attn = sb("attn", [P, 2, 2, D])
        attn_t = sb("attn_t", [P, 4, KC, P])
        wo = sb("wo", [P, KC, D])
        bo_b = sb("bo_b", [P, D])
        rw = sb("rw", [P, KC, EXPERTS])
        rb = sb("rb", [P, EXPERTS])
        stats2 = sb("stats2", [P, TT, 6])
        mv2 = sb("mv2", [P, TT, 2])
        var2 = sb("var2", [P, TT])
        sd2 = sb("sd2", [P, TT])
        rs2 = sb("rs2", [P, 4, TT])
        xn2t = sb("xn2t", [P, 2, KC, P])
        bias = sb("bias", [P, B1 + B2])
        bias3 = sb("bias3", [P, NPART, B1 + B2], BF16)
        b1s = sb("b1s", [NPART * EXPERTS, 2 * HID], BF16)
        b2s = sb("b2s", [NPART * EXPERTS, D], BF16)
        pick_f = attn[0:NPART * EXPERTS, :, :, :].rearrange("r a b d -> r (a b d)").rearrange("r (e n) -> r e n", n=P)
        pick = sb("pick", [NPART * EXPERTS, EXPERTS, P], BF16)
        below = sb("below", [P, P])
        ones = sb("ones", [P, P])
        ints = sb("ints", [P, EXPERTS + TT * EXPERTS + BLOCKS], I32)
        floats = sb("floats", [P, EXPERTS + TT * EXPERTS + BLOCKS])
        route = sb("route", [P, 6, TT, EXPERTS])
        best = sb("best", [P, 2, TT])
        past = sb("past", [P, 6, EXPERTS])
        over = sb("over", [P, EXPERTS, TT])
        slot_f = sb("slot_f", [P, TT])
        slot = sb("slot", [P, TT], U32)
        later = sb("later", [P, BLOCKS, EXPERTS - 1])
        block_f = sb("block_f", [P, 4, BLOCKS])
        block_i = sb("block_i", [P, 2, BLOCKS], I32)
        start_i = sb("start_i", [P, EXPERTS], I32)
        x_now = sb("x_now", [P, D])
        w1s = sb("w1s", [P, WSLOTS, KC, 2 * HID])
        w2s = sb("w2s", [P, WSLOTS, HID // P, D])
        psum = ctx.enter_context(nc.psum_tensor("psum3", [P, 8, 512], F32))

        weights_in = sem("weights_in")
        h_back = sem("h_back")
        made = sem("made")
        bias_added = sem("bias_added")
        zeroed = sem("zeroed")
        step = sem("step")
        attn_ready = sem("attn_ready")
        attn_turned = sem("attn_turned")
        attn_out = sem("attn_out")
        o_made = sem("o_made")
        h_added = sem("h_added")
        var2_ready = sem("var2_ready")
        sd2_done = sem("sd2_done")
        normed = sem("normed")
        xn_turned = sem("xn_turned")
        xn_out = sem("xn_out")
        logits_done = sem("logits_done")
        chosen = sem("chosen")
        counted = sem("counted")
        slots_ready = sem("slots_ready")
        bias_split = sem("bias_split")
        bias_sent = sem("bias_sent")
        bias_back = sem("bias_back")
        scattered = sem("scattered")
        xs_first = sem("xs_first")
        xs_in = sem("xs_in")
        blocks_ready = sem("blocks_ready")
        w_slot = [sem(f"w_slot{i}") for i in range(WSLOTS)]
        experts_in = sem("experts_in")
        x_picked = sem("x_picked")
        xs_turned = sem("xs_turned")
        xs_out = sem("xs_out")
        h_made = sem("h_made")
        exp3_done = sem("exp3_done")
        gate_step = sem("gate_step")
        gated = sem("gated")
        u_turned = sem("u_turned")
        u_out = sem("u_out")
        y_made = sem("y_made")
        y_out = sem("y_out")
        y_sent = sem("y_sent")
        y_back = [sem(f"y_back{i}") for i in range(4)]
        final = sem("final")
        out_sent = sem("out_sent")

        yg = xn2
        iota8, thresh, block_no = (floats[:, 0:EXPERTS], floats[:, EXPERTS:EXPERTS * (TT + 1)],
                                   floats[:, EXPERTS * (TT + 1):])

        def rows_of(dram, w, half):
            return dram.rearrange("(m u w q) c -> u w q m c", u=2, w=NWIN, q=WQ)[half, w]

        def tiles_of(sbuf, w, half):
            return sbuf.rearrange("p (w m) c -> p w m c", w=NWIN)[half * WQ:(half + 1) * WQ, w]

        block = ctx.enter_context(nc.Block())

        @block.sync
        def _(sp):
            def load_expert(e):
                sp.dma_start(w1s[:, e % WSLOTS, :, :], w1[e].rearrange("(k p) n -> p k n", p=P)
                             ).then_inc(w_slot[e % WSLOTS], 16)
                sp.dma_start(w2s[:, e % WSLOTS, :, :], w2[e].rearrange("(k p) n -> p k n", p=P)
                             ).then_inc(w_slot[e % WSLOTS], 16)

            sp.dma_start(wo[:, :, :], wo_t.rearrange("(k p) n -> p k n", p=P)).then_inc(weights_in, 16)
            sp.dma_start(bo_b[:, :], bo.rearrange("(a n) -> a n", a=1).broadcast_to([P, D])).then_inc(weights_in, 16)
            sp.dma_start(rw[:, :, :], router_w.rearrange("(k p) n -> p k n", p=P)).then_inc(weights_in, 16)
            sp.dma_start(rb[:, :], router_b.rearrange("(a n) -> a n", a=1).broadcast_to([P, EXPERTS])
                         ).then_inc(weights_in, 16)
            sp.dma_start(bias[:, 0:B1], b1.rearrange("e (a n) -> (e a) n", n=B1)).then_inc(weights_in, 16)
            sp.dma_start(bias[:, B1:], b2.rearrange("e (a n) -> (e a) n", n=B2)).then_inc(weights_in, 16)
            for w in range(NWIN):
                for half in range(2):
                    sp.dma_start(tiles_of(h2, w, half), rows_of(h_dram, w, half)).then_inc(h_back, 16)
            for e in range(WSLOTS):
                load_expert(e)
            sp.wait_ge(bias_split, 1)
            for a in range(NPART):
                sp.dma_start(b1p_dram[a].rearrange("(p n) -> p n", p=P), bias3[:, a, 0:B1]).then_inc(bias_sent, 16)
                sp.dma_start(b2p_dram[a].rearrange("(p n) -> p n", p=P), bias3[:, a, B1:]).then_inc(bias_sent, 16)
            sp.wait_ge(bias_sent, 16 * 2 * NPART)
            sp.dma_start(b1s[:, :], b1p_dram.rearrange("a (e n) -> (a e) n", e=EXPERTS)).then_inc(bias_back, 16)
            sp.dma_start(b2s[:, :], b2p_dram.rearrange("a (e n) -> (a e) n", e=EXPERTS)).then_inc(bias_back, 16)
            sp.wait_ge(scattered, 16 * TT)
            sp.dma_start(xs[:, 0, :], xs_dram[0:P, :]).then_inc(xs_first, 16)
            sp.dma_start(xs[:, 1:, :], xs_dram[P:, :].rearrange("(k p) c -> p k c", p=P)).then_inc(xs_in, 16)
            sp.wait_ge(blocks_ready, 1)
            for e in range(WSLOTS, EXPERTS):
                sp.wait_ge(y_made, sp.value_load(start_i[0:1, e - WSLOTS + 1:e - WSLOTS + 2], min_val=1, max_val=BLOCKS))
                load_expert(e)
            for w in range(NWIN):
                sp.wait_ge(final, 4 * (w + 1))
                for half in range(2):
                    sp.dma_start(rows_of(out, w, half), tiles_of(h2, w, half)).then_inc(out_sent, 16)
            sp.wait_ge(out_sent, 16 * 2 * NWIN)

        @block.gpsimd
        def _(pool):
            pool.memset(zeros[:, :], 0.0).then_inc(made, 1)
            pool.memset(ones[:, :], 1.0).then_inc(made, 1)
            pool.memset(pick_f[:, :, :], 0.0).then_inc(made, 1)
            pool.iota(ints[:, 0:EXPERTS], pattern=[[1, EXPERTS]], base=0, channel_multiplier=0).then_inc(made, 1)
            pool.iota(ints[:, EXPERTS:EXPERTS * (TT + 1)], pattern=[[0, EXPERTS], [P, TT]], base=0,
                      channel_multiplier=0).then_inc(made, 1)
            pool.iota(ints[:, EXPERTS * (TT + 1):], pattern=[[1, BLOCKS]], base=0, channel_multiplier=0).then_inc(made, 1)
            pool.wait_ge(made, 6)
            pool.dma_start(xs_dram.rearrange("(k p) c -> p k c", p=P),
                           zeros[:, :].unsqueeze(1).broadcast_to([P, BLOCKS, D])).then_inc(zeroed, 16)
            pool.affine_select(out=below[:, :], in_=ones[:, :], compare_op=ALU.is_ge, fill=0.0, base=-1,
                               pattern=[[1, P]], channel_multiplier=-1).then_inc(made, 1)
            for a in range(NPART):
                pool.affine_select(out=pick_f[:, :, :], in_=pick_f[:, :, :], compare_op=ALU.not_equal, fill=1.0,
                                   base=-EXPERTS * a, pattern=[[-1, EXPERTS], [0, P]],
                                   channel_multiplier=1).then_inc(made, 1)
                pool.wait_ge(made, 8 + a)
            pool.wait_ge(weights_in, 16 * 6)
            pool.wait_ge(h_back, 16 * 2 * NWIN)
            for i in range(TT):
                pool.tensor_tensor(h2[:, i, :], h2[:, i, :], bo_b[:, :], ALU.add).then_inc(bias_added, 1)
            pool.wait_ge(zeroed, 16)
            pool.wait_ge(slots_ready, 1)
            for i in range(TT):
                pool.indirect_dma_start(xs_dram, bass.IndirectOffsetOnAxis(slot[:, i:i + 1], 0), xn2[:, i, :],
                                        None).then_inc(scattered, 16)
            for e in range(EXPERTS):
                pool.wait_ge(w_slot[e % WSLOTS], 32 * (e // WSLOTS + 1))
                pool.engine_nop().then_inc(experts_in, 1)
            pool.wait_ge(scattered, 16 * TT)
            pool.wait_ge(y_sent, 16 * BLOCKS)
            for i in range(TT):
                pool.indirect_dma_start(yg[:, i, :], None, ys_dram, bass.IndirectOffsetOnAxis(slot[:, i:i + 1], 0)
                                        ).then_inc(y_back[i // 4], 16)

        @block.tensor
        def _(pe):
            pe.wait_ge(weights_in, 16 * 6)
            for n in range(WINDOWS + 2):
                if n < WINDOWS:
                    pe.wait_ge(attn_ready, n + 1)
                    for i in (2 * n, 2 * n + 1):
                        if i >= 2:
                            pe.wait_ge(attn_out, i - 1)
                        for c in range(KC):
                            ins = pe.transpose(psum[:, i % 2, c * P:(c + 1) * P], attn[:, n % 2, i % 2, c * P:(c + 1) * P],
                                               ident[:, :])
                        ins.then_inc(attn_turned, 1)
                if 1 <= n <= WINDOWS:
                    for i in (2 * n - 2, 2 * n - 1):
                        pe.wait_ge(attn_out, i + 1)
                        if i >= 2:
                            pe.wait_ge(h_added, i - 1)
                        for c in range(KC):
                            ins = pe.matmul(psum[:, 2 + i % 2, 0:D], attn_t[:, i % 4, c, :], wo[:, c, :],
                                            start=(c == 0), stop=(c == KC - 1))
                        ins.then_inc(o_made, 1)

                def turn_normed(i):
                    pe.wait_ge(normed, i + 1)
                    if i >= 2:
                        pe.wait_ge(xn_out, i - 1)
                    for c in range(KC):
                        ins = pe.transpose(psum[:, 4 + i % 2, c * P:(c + 1) * P], xn2[:, i, c * P:(c + 1) * P],
                                           ident[:, :])
                    ins.then_inc(xn_turned, 1)

                if n >= 3 and n % 2:
                    first = 2 * n - 2 - LN_GROUP
                    turn_normed(first)
                    for i in range(first, first + LN_GROUP):
                        if i + 1 < first + LN_GROUP:
                            turn_normed(i + 1)
                        pe.wait_ge(xn_out, i + 1)
                        for c in range(KC):
                            ins = pe.matmul(psum[:, 6, i * EXPERTS:(i + 1) * EXPERTS], xn2t[:, i % 2, c, :], rw[:, c, :],
                                            start=(c == 0), stop=(c == KC - 1))
                        ins.then_inc(logits_done, 1)
            pe.wait_ge(made, 7)
            pe.wait_ge(chosen, 1)
            hot = route[:, 2, :, :].rearrange("p t e -> p (t e)")
            pe.matmul(psum[:, 7, 0:P], below[:, :], hot, start=True, stop=True)
            pe.matmul(psum[:, 7, P:2 * P], ones[:, :], hot, start=True, stop=True).then_inc(counted, 1)

            pe.wait_ge(bias_back, 32)
            pe.wait_ge(blocks_ready, 1)

            def turn_tokens(ahead):
                x_picked_.wait_ge(ahead + 1)
                for c in range(KC):
                    ins = pe.transpose(psum[:, 7, c * P:(c + 1) * P], x_now[:, c * P:(c + 1) * P], ident[:, :])
                ins.then_inc(xs_turned, 1)

            def hidden(e, ws, half):
                for part in range(2):
                    cols = part * HID + half * HH
                    bank = 2 * half + part
                    pe.matmul(psum[:, bank, :], pick[:, bass.ds(e, 1), :].rearrange("r o p -> r (o p)"),
                              b1s[:, cols:cols + HH], start=True, stop=False)
                    for c in range(KC):
                        ins = pe.matmul(psum[:, bank, :], xst[:, c, :],
                                        w1s[:, bass.ds(ws, 1), c, cols:cols + HH].rearrange("p o n -> p (o n)"),
                                        start=False, stop=(c == KC - 1))
                ins.then_inc(h_made, 1)

            def turn_units(half):
                for c in range(HC):
                    ins = pe.transpose(psum[:, 4 + half, c * P:(c + 1) * P], u[:, half, c * P:(c + 1) * P], ident[:, :])
                ins.then_inc(u_turned, 1)

            def output(e, ws, half):
                if half == 0:
                    pe.matmul(psum[:, 6, 0:D], pick[:, bass.ds(e, 1), :].rearrange("r o p -> r (o p)"), b2s[:, :],
                              start=True, stop=False)
                for c in range(HC):
                    ins = pe.matmul(psum[:, 6, 0:D], ut[:, half, c, :],
                                    w2s[:, bass.ds(ws, 1), half * HC + c, :].rearrange("p o n -> p (o n)"),
                                    start=False, stop=(half == 1 and c == HC - 1))
                if half:
                    ins.then_inc(y_made, 1)

            xs_out_, gated_ = Awaited(pe, xs_out, 1), Awaited(pe, gated, HALVES)
            u_out_, y_out_ = Awaited(pe, u_out, HALVES), Awaited(pe, y_out, 1, ONE)
            x_picked_ = Awaited(pe, x_picked, 1)
            awaited_all = (xs_out_, gated_, u_out_, y_out_, x_picked_)

            def expert_of(k):
                return (pe.value_load(block_i[0:1, 0, bass.ds(k, 1)], min_val=0, max_val=EXPERTS - 1),
                        pe.value_load(block_i[0:1, 1, bass.ds(k, 1)], min_val=0, max_val=WSLOTS - 1))

            def finish(e, ws, between):
                gated_.wait_ge(0)
                turn_units(1)
                u_out_.wait_ge(-1)
                y_out_.wait_ge(-1)
                output(e, ws, 0)
                between()
                u_out_.wait_ge(0)
                output(e, ws, 1)

            def block_steps(k, first=False, last=False):
                e, ws = expert_of(k)
                pe.wait_ge(experts_in, e + 1)
                xs_out_.wait_ge(1)
                hidden(e, ws, 0)

                def second_half():
                    hidden(e, ws, 1)
                    if not last:
                        turn_tokens(1)
                    gated_.wait_ge(1)
                    turn_units(0)

                if first:
                    second_half()
                else:
                    finish(*expert_of(k - 1), second_half)
                for awaited in awaited_all:
                    awaited.next_turn()

            turn_tokens(0)
            block_steps(0, first=True)
            for awaited in awaited_all:
                awaited.enter_loop()
            with pe.Fori(1, BLOCKS - 1) as k:
                block_steps(k)
            block_steps(BLOCKS - 1, last=True)
            finish(*expert_of(BLOCKS - 1), lambda: None)

        @block.scalar
        def _(act):
            for n in range(WINDOWS + 2):
                if n < WINDOWS:
                    for i in (2 * n, 2 * n + 1):
                        act.wait_ge(attn_turned, i + 1)
                        if i >= 4:
                            act.wait_ge(o_made, i - 3)
                        act.activation(attn_t[:, i % 4, :, :], psum[:, i % 2, 0:D].rearrange("p (c n) -> p c n", c=KC),
                                       ACT.Copy).then_inc(attn_out, 1)
                if n >= 2 and n % 2 == 0 and n <= WINDOWS:
                    tiles = slice(2 * n - LN_GROUP, 2 * n)
                    act.wait_ge(var2_ready, n // 2)
                    act.activation(sd2[:, tiles], var2[:, tiles], ACT.Sqrt).then_inc(sd2_done, 1)
                if n >= 3 and n % 2:
                    for i in range(2 * n - 2 - LN_GROUP, 2 * n - 2):
                        act.wait_ge(xn_turned, i + 1)
                        if i >= 2:
                            act.wait_ge(logits_done, i - 1)
                        act.activation(xn2t[:, i % 2, :, :], psum[:, 4 + i % 2, 0:D].rearrange("p (c n) -> p c n", c=KC),
                                       ACT.Copy).then_inc(xn_out, 1)

            h_made_, u_turned_ = Awaited(act, h_made, HALVES), Awaited(act, u_turned, HALVES)
            xs_turned_, y_made_, y_out_ = Awaited(act, xs_turned, 1), Awaited(act, y_made, 1), Awaited(act, y_out, 1, ONE)
            awaited_all = (h_made_, u_turned_, xs_turned_, y_made_, y_out_)

            def exponents(half):
                h_made_.wait_ge(half + 1)
                act.activation(eg[:, half, :], psum[:, 2 * half + 1, :], ACT.Exp, scale=-1.0).then_inc(exp3_done, 1)

            def tokens_out():
                act.activation(xst[:, :, :], psum[:, 7, 0:D].rearrange("p (c n) -> p c n", c=KC), ACT.Copy
                               ).then_inc(xs_out, 1)

            def units_out(half):
                act.activation(ut[:, half, :, :], psum[:, 4 + half, :].rearrange("p (c n) -> p c n", c=HC), ACT.Copy
                               ).then_inc(u_out, 1)

            def outputs_out(k):
                y_made_.wait_ge(0)
                act.activation(xs[:, bass.ds(k, 1), :].rearrange("p o c -> p (o c)"), psum[:, 6, 0:D], ACT.Copy
                               ).then_inc(y_out, 1)
                y_out_.wait_ge(0)
                act.dma_start(ys_dram[bass.ds(k * P, P), :], xs[:, bass.ds(k, 1), :].rearrange("p o c -> p (o c)")
                              ).then_inc(y_sent, 16)

            def block_steps(k, first=False, last=False):
                exponents(0)
                if not first:
                    u_turned_.wait_ge(0)
                    units_out(1)
                exponents(1)
                if not last:
                    xs_turned_.wait_ge(2)
                    tokens_out()
                u_turned_.wait_ge(1)
                units_out(0)
                if not first:
                    outputs_out(k - 1)
                for awaited in awaited_all:
                    awaited.next_turn()

            xs_turned_.wait_ge(1)
            tokens_out()
            block_steps(0, first=True)
            for awaited in awaited_all:
                awaited.enter_loop()
            with act.Fori(1, BLOCKS - 1) as k:
                block_steps(k)
            block_steps(BLOCKS - 1, last=True)
            u_turned_.wait_ge(0)
            units_out(1)
            outputs_out(BLOCKS - 1)

        @block.vector
        def _(dve):
            n_steps = [0]
            dve.engine_nop().then_inc(y_out, ONE)

            def follow(ins):
                n_steps[0] += 1
                ins.then_inc(step, 1)
                dve.wait_ge(step, n_steps[0])

            def normalise(tiles):
                for i in tiles:
                    ins = dve.bn_stats(stats2[:, i, :], h2[:, i, :])
                    if i < tiles[-1]:
                        ins.then_inc(step, 1)
                        n_steps[0] += 1
                follow(ins)
                for i in tiles:
                    ins = dve.bn_aggr(mv2[:, i, :], stats2[:, i, :])
                    if i < tiles[-1]:
                        ins.then_inc(step, 1)
                        n_steps[0] += 1
                follow(ins)
                g = slice(tiles[0], tiles[-1] + 1)
                dve.tensor_scalar(var2[:, g], mv2[:, g, 1], EPS, None, ALU.add).then_inc(var2_ready, 1)
                dve.wait_ge(sd2_done, tiles[0] // LN_GROUP + 1)
                follow(dve.reciprocal(rs2[:, 0, g], sd2[:, g]))
                follow(dve.tensor_tensor(rs2[:, 1, g], rs2[:, 0, g], rs2[:, 0, g], ALU.mult))
                follow(dve.tensor_tensor(rs2[:, 2, g], rs2[:, 1, g], var2[:, g], ALU.mult))
                follow(dve.tensor_scalar(rs2[:, 1, g], rs2[:, 2, g], -0.5, 1.5, ALU.mult, ALU.add))
                follow(dve.tensor_tensor(rs2[:, 3, g], rs2[:, 0, g], rs2[:, 1, g], ALU.mult))
                for i in tiles:
                    dve.tensor_scalar(xn2[:, i, :], h2[:, i, :], mv2[:, i, 0:1], rs2[:, 3, i:i + 1],
                                      ALU.subtract, ALU.mult).then_inc(normed, 1)

            dve.wait_ge(made, 10)
            follow(dve.tensor_copy(pick[:, :, :], pick_f))
            follow(dve.reciprocal(rec[:, :, :], sums[:, 0:WINDOWS, :]))
            dve.wait_ge(weights_in, 16 * 6)
            for a in range(NPART):
                ins = dve.tensor_copy(bias3[:, a, :], bias[:, :])
                follow(ins)
                if a < NPART - 1:
                    follow(dve.tensor_tensor(bias[:, :], bias[:, :], bias3[:, a, :], ALU.subtract))
            dve.engine_nop().then_inc(bias_split, 1)
            def divide(n):
                if n >= 2:
                    dve.wait_ge(attn_turned, 2 * (n - 1))
                dve.tensor_tensor(attn[:, n % 2, :, :].rearrange("p m (h d) -> p h m d", d=HD),
                                  o_all[:, n, :, :].rearrange("p (h m) d -> p h m d", m=2),
                                  rec[:, n, :].rearrange("p (h m) -> p h m", m=2).unsqueeze(3).broadcast_to(
                                      [P, HEADS, 2, HD]), ALU.mult).then_inc(attn_ready, 1)

            divide(0)
            for n in range(WINDOWS + 1):
                if n + 1 < WINDOWS:
                    divide(n + 1)
                if n >= 1:
                    for i in (2 * n - 2, 2 * n - 1):
                        dve.wait_ge(o_made, i + 1)
                        dve.wait_ge(bias_added, i + 1)
                        dve.tensor_tensor(h2[:, i, :], psum[:, 2 + i % 2, 0:D], h2[:, i, :], ALU.add).then_inc(h_added, 1)
                if n >= 2 and n % 2 == 0:
                    dve.wait_ge(h_added, 2 * n)
                    normalise(range(2 * n - LN_GROUP, 2 * n))

            def per_tile(ap):
                return ap.unsqueeze(2).broadcast_to([P, TT, EXPERTS])

            def per_expert(ap):
                return ap.unsqueeze(1).broadcast_to([P, TT, EXPERTS])

            logits, cand, hot, acc_a, acc_b, rank = (route[:, i, :, :] for i in range(6))
            follow(dve.tensor_copy(floats[:, :], ints[:, :]))
            dve.wait_ge(logits_done, TT)
            follow(dve.tensor_tensor(logits, psum[:, 6, 0:TT * EXPERTS].rearrange("p (t e) -> p t e", e=EXPERTS),
                                     per_expert(rb[:, :]), ALU.add))
            follow(dve.tensor_reduce(best[:, 0, :], logits, AX.X, ALU.max))
            follow(dve.tensor_tensor(cand, logits, per_tile(best[:, 0, :]), ALU.is_equal))
            follow(dve.tensor_scalar(cand, cand, -100.0, None, ALU.mult))
            follow(dve.tensor_tensor(cand, cand, per_expert(iota8), ALU.add))
            follow(dve.tensor_reduce(best[:, 1, :], cand, AX.X, ALU.min))
            dve.tensor_tensor(hot, cand, per_tile(best[:, 1, :]), ALU.is_equal).then_inc(chosen, 1)
            dve.wait_ge(counted, 1)
            counts = psum[:, 7, P:2 * P].rearrange("p (t e) -> p t e", e=EXPERTS)
            follow(dve.tensor_copy(acc_a, counts))
            src, dst = acc_a, acc_b
            shift = 1
            while shift < TT:
                follow(dve.tensor_copy(dst[:, 0:shift, :], src[:, 0:shift, :]))
                follow(dve.tensor_tensor(dst[:, shift:, :], src[:, shift:, :], src[:, 0:TT - shift, :], ALU.add))
                src, dst = dst, src
                shift *= 2
            follow(dve.tensor_tensor(dst, src, counts, ALU.subtract))
            follow(dve.tensor_tensor(rank, psum[:, 7, 0:P].rearrange("p (t e) -> p t e", e=EXPERTS), dst, ALU.add))
            follow(dve.tensor_tensor(over[:, :, 0:TT - 1], src[:, TT - 1, :].unsqueeze(2).broadcast_to([P, EXPERTS, TT - 1]),
                                     thresh.rearrange("p (e t) -> p e t", e=EXPERTS)[:, :, 1:], ALU.is_gt))
            follow(dve.tensor_reduce(past[:, 1, :], over[:, :, 0:TT - 1], AX.X, ALU.add))
            follow(dve.tensor_scalar(past[:, 0, :], past[:, 1, :], 1.0, None, ALU.add))
            at, shift = 0, 1
            while shift < EXPERTS:
                follow(dve.tensor_copy(past[:, at + 1, 0:shift], past[:, at, 0:shift]))
                follow(dve.tensor_tensor(past[:, at + 1, shift:], past[:, at, shift:], past[:, at, 0:EXPERTS - shift],
                                         ALU.add))
                at, shift = at + 1, 2 * shift
            first = past[:, 4, :]
            follow(dve.tensor_tensor(first, past[:, at, :], past[:, 0, :], ALU.subtract))
            follow(dve.tensor_copy(start_i[:, :], first))
            follow(dve.tensor_scalar(past[:, 5, :], first, float(P), None, ALU.mult))
            follow(dve.tensor_tensor(rank, rank, per_expert(past[:, 5, :]), ALU.add))
            follow(dve.tensor_tensor(rank, rank, hot, ALU.mult))
            follow(dve.tensor_reduce(slot_f[:, :], rank, AX.X, ALU.add))
            dve.tensor_copy(slot[:, :], slot_f[:, :]).then_inc(slots_ready, 1)
            follow(dve.tensor_tensor(later[:, :, :], first[:, 1:].unsqueeze(1).broadcast_to([P, BLOCKS, EXPERTS - 1]),
                                     block_no.unsqueeze(2).broadcast_to([P, BLOCKS, EXPERTS - 1]), ALU.is_le))
            follow(dve.tensor_reduce(block_f[:, 0, :], later[:, :, :], AX.X, ALU.add))
            follow(dve.tensor_scalar(block_f[:, 1, :], block_f[:, 0, :], float(WSLOTS), float(WSLOTS), ALU.is_ge, ALU.mult))
            follow(dve.tensor_tensor(block_f[:, 2, :], block_f[:, 0, :], block_f[:, 1, :], ALU.subtract))
            follow(dve.tensor_copy(block_i[:, 0, :], block_f[:, 0, :]))
            follow(dve.tensor_copy(block_i[:, 1, :], block_f[:, 2, :]))
            dve.engine_nop().then_inc(blocks_ready, 1)

            exp3_done_, gate_step_ = Awaited(dve, exp3_done, HALVES), Awaited(dve, gate_step, 2 * HALVES)
            xs_turned_ = Awaited(dve, xs_turned, 1)

            def block_steps():
                for half in range(HALVES):
                    exp3_done_.wait_ge(half + 1)
                    dve.tensor_scalar(eg[:, half, :], eg[:, half, :], 1.0, None, ALU.add).then_inc(gate_step, 1)
                    gate_step_.wait_ge(2 * half + 1)
                    dve.reciprocal(eg[:, half, :], eg[:, half, :]).then_inc(gate_step, 1)
                    gate_step_.wait_ge(2 * half + 2)
                    dve.tensor_tensor(u[:, half, :], psum[:, 2 * half, :], eg[:, half, :], ALU.mult).then_inc(gated, 1)
                for awaited in (exp3_done_, gate_step_, xs_turned_):
                    awaited.next_turn()

            dve.wait_ge(xs_first, 16)
            dve.tensor_copy(x_now[:, :], xs[:, 0, :]).then_inc(x_picked, 1)
            dve.wait_ge(xs_in, 16)
            for awaited in (exp3_done_, gate_step_, xs_turned_):
                awaited.enter_loop()
            with dve.Fori(0, BLOCKS - 1) as k:
                xs_turned_.wait_ge(1)
                dve.tensor_copy(x_now[:, :], xs[:, bass.ds(k + 1, 1), :].rearrange("p o c -> p (o c)")
                                ).then_inc(x_picked, 1)
                block_steps()
            block_steps()
            for i in range(TT):
                dve.wait_ge(y_back[i // 4], 64)
                dve.tensor_tensor(h2[:, i, :], h2[:, i, :], yg[:, i, :], ALU.add).then_inc(final, 1)


def vit_tower(nc, x, wave_w, wave_b, wq_t, wk_t, wv_t, qkv_b, ext_k, ext_v, wo_t, bo, router_w, router_b, w1, b1, w2,
              b2, out):
    def scratch(name, shape, dt=F32):
        return nc.dram_tensor(name, shape, dt, kind="Internal").ap()

    h_dram = scratch("h_scratch", [TOK, D])
    q_dram = scratch("q_scratch", [WINDOWS, NPART, D, BG, WQ], BF16)
    k_dram = scratch("k_scratch", [NPART, D, B, S], BF16)
    ek_dram = scratch("ek_scratch", [STACK, EXT], BF16)
    ev_dram = scratch("ev_scratch", [EXT, NPART, HD], BF16)
    rel_dram = scratch("rel_scratch", [GROUPS, NB, 2, PAIRS * S])
    rv_dram = scratch("rv_scratch", [WINDOWS, NB, 2, PAIRS * HD])
    b1p_dram = scratch("b1_scratch", [NPART, EXPERTS * 2 * HID], BF16)
    b2p_dram = scratch("b2_scratch", [NPART, EXPERTS * D], BF16)
    xs_dram = scratch("xs_scratch", [BLOCKS * P, D])
    ys_dram = scratch("ys_scratch", [BLOCKS * P, D])
    with ExitStack() as ctx:
        ident = ctx.enter_context(nc.sbuf_tensor("ident", [P, P], F32))
        o_all = ctx.enter_context(nc.sbuf_tensor("o_all", [P, WINDOWS, TILES, HD], F32))
        sums = ctx.enter_context(nc.sbuf_tensor("sums", [P, WINDOWS + 1, TILES], F32))
        with nc.sbuf_tensor("v_parts", [P, NPART, KC, B, D], BF16) as v_parts:
            tokens_stage(nc, x, wave_w, wave_b, wq_t, wk_t, wv_t, qkv_b, ext_k, ext_v, h_dram, v_parts, q_dram, k_dram,
                         ek_dram, ev_dram, ident)
            attention_stage(nc, q_dram, k_dram, ek_dram, ev_dram, rel_dram, rv_dram, v_parts, ident, o_all, sums)
        feed_forward_stage(nc, h_dram, o_all, sums, ident, wo_t, bo, router_w, router_b, w1, b1, w2, b2,
                           b1p_dram, b2p_dram, xs_dram, ys_dram, out)


def lay_out(given):
    rows = S // ROWS
    wave = [given["L0_tok_Wa"].reshape(rows, -1)]
    for level in (1, 2, 3):
        w = given[f"L0_tok_Wd{level}"]
        wave.append(w.reshape(3, rows, -1, 3).transpose(1, 3, 0, 2).reshape(rows, -1))
    shift = np.arange(EXT)
    reach = (given["L0_attn_rel_k"].shape[0] - 1) // 2
    rows = np.clip(shift - (S - 1), -reach, reach) + reach
    laid = {
        "x": given["x"],
        "wave_w": np.concatenate(wave, axis=1),
        "wave_b": np.concatenate([given[f"L0_tok_{n}"] for n in ("ba", "bd1", "bd2", "bd3")]),
        "wq_t": given["L0_attn_Wq"].T,
        "wk_t": given["L0_attn_Wk"].T,
        "wv_t": given["L0_attn_Wv"].T,
        "qkv_b": np.stack([given["L0_attn_bq"], given["L0_attn_bk"], given["L0_attn_bv"]]),
        "ext_k": given["L0_attn_rel_k"][rows].T,
        "ext_v": given["L0_attn_rel_v"][rows],
        "wo_t": given["L0_attn_Wo"].T,
        "bo": given["L0_attn_bo"],
    }
    for n in ("router_w", "router_b", "w1", "b1", "w2", "b2"):
        laid[n] = given[f"L0_ffn_{n}"]
    return {n: np.ascontiguousarray(a) for n, a in laid.items()}


def kernel(**inputs):
    import concourse.bacc as bacc
    from concourse.bass_utils import run_bass_kernel_spmd

    arrays = lay_out({n: np.asarray(a) for n, a in inputs.items()})
    nc = bacc.Bacc("TRN2", target_bir_lowering=False, num_devices=1)
    args = [nc.dram_tensor("in_" + n, a.shape, mybir.dt.from_np(a.dtype), kind="ExternalInput").ap()
            for n, a in arrays.items()]
    args.append(nc.dram_tensor("out", [TOK, D], F32, kind="ExternalOutput").ap())
    vit_tower(nc, *args)
    result = run_bass_kernel_spmd(nc, [{"in_" + n: a for n, a in arrays.items()}], core_ids=[0])
    return result.results[0]["out"].reshape(B, S, D)
```
